# Optimizing a Trainium2 kernel written in Bass

```python
import numpy as np
import jax
import jax.numpy as jnp

def _softmax(x, axis=-1):
    return jax.nn.softmax(x, axis=axis)

def _gelu(x):
    return jax.nn.gelu(x, approximate=True)

def _silu(x):
    return jax.nn.silu(x)

def _sigmoid(x):
    return jax.nn.sigmoid(x)

def _layernorm(x, axis=-1, eps=1e-05):
    m = jnp.mean(x, axis=axis, keepdims=True)
    v = jnp.var(x, axis=axis, keepdims=True)
    return (x - m) / jnp.sqrt(v + eps)

def _scatter_add(tgt, idx, src, axis=0):
    return tgt.at[idx].add(src)

def _segment_sum(src, seg, n):
    return jax.ops.segment_sum(src, seg, n)
kernel_name = 'mk_adaln_attn_ffn_d1_seqx_r8_0e911f'

def setup_inputs(seed: int=0):
    np.random.seed(seed)
    _w = jnp.asarray

    def _rec_inputs():
        import jax
        import jax.numpy as jnp
        _rk = jax.random.key(seed)
        x = -7.109e-05 + 0.9999 * jax.random.normal(jax.random.fold_in(_rk, 1), (32, 32, 128), jnp.float32)
        _lenS = 32 - jax.random.randint(jax.random.fold_in(_rk, 7), (32,), 0, max(1, 32 // 4) + 1, jnp.int32)
        _lenS2 = 32 - jax.random.randint(jax.random.fold_in(_rk, 8), (32,), 0, max(1, 32 // 4) + 1, jnp.int32)
        itok_B_0_15 = jax.random.randint(jax.random.fold_in(_rk, 11), (32,), 0, 16, jnp.int32)
        itok_B_0_2 = jax.random.randint(jax.random.fold_in(_rk, 12), (32,), 0, 3, jnp.int32)
        return (x, itok_B_0_15, itok_B_0_2)
    x, itok_B_0_15, itok_B_0_2 = _rec_inputs()

    def _L0_cond_setup():
        import jax, jax.numpy as jnp
        import numpy as np
        B, N, C_IN, C_OUT, S = (64, 128, 128, 128, 16)
        key = jax.random.key(seed)
        kx, ks, kw, kb = jax.random.split(key, 4)
        scale = 1.0 / np.sqrt(C_IN)
        x = jax.random.normal(kx, (B, N, C_IN), dtype=jnp.float32)
        subjects = jax.random.randint(ks, (B,), 0, S, dtype=jnp.int64)
        weights = jax.random.normal(kw, (S, C_IN, C_OUT), dtype=jnp.float32) * scale
        b = jax.random.normal(kb, (S, C_OUT), dtype=jnp.float32) * scale
        return {'x': x, 'subjects': subjects, 'weights': weights, 'b': b}
    _L0_cond_all = _L0_cond_setup()
    _L0_cond_in = {k: v for k, v in _L0_cond_all.items() if k in ('weights', 'b')}
    del _L0_cond_all

    def _L0_attn_setup():
        import jax, jax.numpy as jnp
        import numpy as np
        from jax import lax
        B, T, H, D = (8, 256, 128, 128)
        RMS_EPS = 1e-08

        def rms_norm(x, w):
            var = jnp.mean(jnp.square(x), axis=-1, keepdims=True)
            return x * lax.rsqrt(var + RMS_EPS) * w

        def act_quant(x):
            scale = 127.0 / jnp.clip(jnp.max(jnp.abs(x), axis=-1, keepdims=True), 1e-05, None)
            return jnp.clip(jnp.round(x * scale), -128, 127) / scale

        def weight_quant(w):
            scale = 1.0 / jnp.clip(jnp.mean(jnp.abs(w)), 1e-05, None)
            return jnp.clip(jnp.round(w * scale), -1, 1) / scale

        def bit_linear(x, w, rms_w):
            xn = rms_norm(x, rms_w)
            xq = xn + lax.stop_gradient(act_quant(xn) - xn)
            wq = w + lax.stop_gradient(weight_quant(w) - w)
            return xq @ wq.T

        def wkv_with_eps(time_decay, time_first, k, v):
            w_log = -jnp.exp(time_decay)
            u = time_first
            Bz, Tz, Dz = k.shape
            init = (jnp.zeros((Bz, Dz), k.dtype), jnp.zeros((Bz, Dz), k.dtype), jnp.zeros((Bz, Dz), k.dtype))

            def step(carry, kv):
                alpha, beta, eps = carry
                kt, vt = kv
                ukt = u + kt
                tau = jnp.maximum(ukt, eps)
                e1 = jnp.exp(eps - tau)
                e2 = jnp.exp(ukt - tau)
                out = (e1 * alpha + e2 * vt) / (e1 * beta + e2)
                w_eps = eps + w_log
                eps_n = jnp.maximum(w_eps, kt)
                e1n = jnp.exp(w_eps - eps_n)
                e2n = jnp.exp(kt - eps_n)
                return ((e1n * alpha + e2n * vt, e1n * beta + e2n, eps_n), out)
            _, outs = lax.scan(step, init, (jnp.swapaxes(k, 0, 1), jnp.swapaxes(v, 0, 1)))
            return jnp.swapaxes(outs, 0, 1)
        key = jax.random.key(seed)
        ks = jax.random.split(key, 16)
        std = 0.02
        return {'hidden': jax.random.normal(ks[0], (B, T, H), jnp.float32), 'time_decay': jax.random.normal(ks[1], (D,), jnp.float32), 'time_first': jax.random.normal(ks[2], (D,), jnp.float32), 'time_mix_key': jax.random.uniform(ks[3], (1, 1, H), jnp.float32), 'time_mix_value': jax.random.uniform(ks[4], (1, 1, H), jnp.float32), 'time_mix_receptance': jax.random.uniform(ks[5], (1, 1, H), jnp.float32), 'w_key': std * jax.random.normal(ks[6], (D, H), jnp.float32), 'w_value': std * jax.random.normal(ks[7], (D, H), jnp.float32), 'w_receptance': std * jax.random.normal(ks[8], (D, H), jnp.float32), 'w_output': std * np.sqrt(1.0 / 2 * 24) * jax.random.normal(ks[9], (H, D), jnp.float32), 'rms_key': jnp.ones((H,), jnp.float32), 'rms_value': jnp.ones((H,), jnp.float32), 'rms_receptance': jnp.ones((H,), jnp.float32), 'rms_output': jnp.ones((D,), jnp.float32)}
    _L0_attn_all = _L0_attn_setup()
    _L0_attn_in = {k: v for k, v in _L0_attn_all.items() if k in ('time_decay', 'time_first', 'time_mix_key', 'time_mix_value', 'time_mix_receptance', 'w_key', 'w_value', 'w_receptance', 'w_output', 'rms_key', 'rms_value', 'rms_receptance', 'rms_output')}
    del _L0_attn_all

    def _L0_cond2_setup():
        import jax, jax.numpy as jnp
        import numpy as np
        NEG_INF = -1e+30
        key = jax.random.key(seed)
        k1, k2, k3, k4, k5 = jax.random.split(key, 5)
        B, S, D, A = (16, 128, 128, 32)
        hidden = jax.random.normal(k1, (B, S, D), dtype=jnp.float32)
        W1 = jax.random.normal(k2, (D, A), dtype=jnp.float32) / np.sqrt(D)
        b1 = jax.random.normal(k3, (A,), dtype=jnp.float32) * 0.01
        v = jax.random.normal(k4, (A,), dtype=jnp.float32) / np.sqrt(A)
        prompt_type_ids = jax.random.randint(k5, (B,), 0, 3, dtype=jnp.int32)
        return {'hidden': hidden, 'W1': W1, 'b1': b1, 'v': v, 'prompt_type_ids': prompt_type_ids}
    _L0_cond2_all = _L0_cond2_setup()
    _L0_cond2_in = {k: v for k, v in _L0_cond2_all.items() if k in ('W1', 'b1', 'v')}
    del _L0_cond2_all

    def _L0_ffn_setup():
        import jax, jax.numpy as jnp
        import numpy as np
        DIM = 128
        HID = 352
        N_ROUTED = 7
        TOPK = 2
        B, S = (4, 256)

        def _expert(x, wg, wu, wd):
            return jax.nn.silu(x @ wg) * (x @ wu) @ wd
        key = jax.random.key(seed)
        ks = jax.random.split(key, 9)
        s = 0.02
        x = jax.random.normal(ks[0], (B, S, DIM), jnp.float32)
        shared_gate = jax.random.normal(ks[1], (DIM, HID), jnp.float32) * s
        shared_up = jax.random.normal(ks[2], (DIM, HID), jnp.float32) * s
        shared_down = jax.random.normal(ks[3], (HID, DIM), jnp.float32) * s
        routed_gate = jax.random.normal(ks[4], (N_ROUTED, DIM, HID), jnp.float32) * s
        routed_up = jax.random.normal(ks[5], (N_ROUTED, DIM, HID), jnp.float32) * s
        routed_down = jax.random.normal(ks[6], (N_ROUTED, HID, DIM), jnp.float32) * s
        Wr = jax.random.normal(ks[7], (DIM, N_ROUTED), jnp.float32) * s
        routing_bias = jax.random.normal(ks[8], (N_ROUTED,), jnp.float32)
        return dict(x=x, shared_gate=shared_gate, shared_up=shared_up, shared_down=shared_down, routed_gate=routed_gate, routed_up=routed_up, routed_down=routed_down, Wr=Wr, routing_bias=routing_bias)
    _L0_ffn_all = _L0_ffn_setup()
    _L0_ffn_in = {k: v for k, v in _L0_ffn_all.items() if k in ('shared_gate', 'shared_up', 'shared_down', 'routed_gate', 'routed_up', 'routed_down', 'Wr', 'routing_bias')}
    del _L0_ffn_all
    return {'x': x, 'itok_B_0_15': itok_B_0_15, 'itok_B_0_2': itok_B_0_2, 'L0_cond_weights': _L0_cond_in['weights'], 'L0_cond_b': _L0_cond_in['b'], 'L0_attn_time_decay': _L0_attn_in['time_decay'], 'L0_attn_time_first': _L0_attn_in['time_first'], 'L0_attn_time_mix_key': _L0_attn_in['time_mix_key'], 'L0_attn_time_mix_value': _L0_attn_in['time_mix_value'], 'L0_attn_time_mix_receptance': _L0_attn_in['time_mix_receptance'], 'L0_attn_w_key': _L0_attn_in['w_key'], 'L0_attn_w_value': _L0_attn_in['w_value'], 'L0_attn_w_receptance': _L0_attn_in['w_receptance'], 'L0_attn_w_output': _L0_attn_in['w_output'], 'L0_attn_rms_key': _L0_attn_in['rms_key'], 'L0_attn_rms_value': _L0_attn_in['rms_value'], 'L0_attn_rms_receptance': _L0_attn_in['rms_receptance'], 'L0_attn_rms_output': _L0_attn_in['rms_output'], 'L0_cond2_W1': _L0_cond2_in['W1'], 'L0_cond2_b1': _L0_cond2_in['b1'], 'L0_cond2_v': _L0_cond2_in['v'], 'L0_ffn_shared_gate': _L0_ffn_in['shared_gate'], 'L0_ffn_shared_up': _L0_ffn_in['shared_up'], 'L0_ffn_shared_down': _L0_ffn_in['shared_down'], 'L0_ffn_routed_gate': _L0_ffn_in['routed_gate'], 'L0_ffn_routed_up': _L0_ffn_in['routed_up'], 'L0_ffn_routed_down': _L0_ffn_in['routed_down'], 'L0_ffn_Wr': _L0_ffn_in['Wr'], 'L0_ffn_routing_bias': _L0_ffn_in['routing_bias']}

def reference(x, itok_B_0_15, itok_B_0_2, L0_cond_weights, L0_cond_b, L0_attn_time_decay, L0_attn_time_first, L0_attn_time_mix_key, L0_attn_time_mix_value, L0_attn_time_mix_receptance, L0_attn_w_key, L0_attn_w_value, L0_attn_w_receptance, L0_attn_w_output, L0_attn_rms_key, L0_attn_rms_value, L0_attn_rms_receptance, L0_attn_rms_output, L0_cond2_W1, L0_cond2_b1, L0_cond2_v, L0_ffn_shared_gate, L0_ffn_shared_up, L0_ffn_shared_down, L0_ffn_routed_gate, L0_ffn_routed_up, L0_ffn_routed_down, L0_ffn_Wr, L0_ffn_routing_bias):
    import jax
    import jax.numpy as jnp

    def _L0_cond_ref(x, subjects, weights, b):
        import jax, jax.numpy as jnp
        import numpy as np
        B, N, C_IN, C_OUT, S = (64, 128, 128, 128, 16)
        w = weights[subjects]
        out = jnp.einsum('bnc,bcd->bnd', x, w)
        out = out + b[subjects][:, None, :]
        return out

    def _L0_attn_ref(hidden, time_decay, time_first, time_mix_key, time_mix_value, time_mix_receptance, w_key, w_value, w_receptance, w_output, rms_key, rms_value, rms_receptance, rms_output):
        import jax, jax.numpy as jnp
        import numpy as np
        from jax import lax
        B, T, H, D = (8, 256, 128, 128)
        RMS_EPS = 1e-08

        def rms_norm(x, w):
            var = jnp.mean(jnp.square(x), axis=-1, keepdims=True)
            return x * lax.rsqrt(var + RMS_EPS) * w

        def act_quant(x):
            scale = 127.0 / jnp.clip(jnp.max(jnp.abs(x), axis=-1, keepdims=True), 1e-05, None)
            return jnp.clip(jnp.round(x * scale), -128, 127) / scale

        def weight_quant(w):
            scale = 1.0 / jnp.clip(jnp.mean(jnp.abs(w)), 1e-05, None)
            return jnp.clip(jnp.round(w * scale), -1, 1) / scale

        def bit_linear(x, w, rms_w):
            xn = rms_norm(x, rms_w)
            xq = xn + lax.stop_gradient(act_quant(xn) - xn)
            wq = w + lax.stop_gradient(weight_quant(w) - w)
            return xq @ wq.T

        def wkv_with_eps(time_decay, time_first, k, v):
            w_log = -jnp.exp(time_decay)
            u = time_first
            Bz, Tz, Dz = k.shape
            init = (jnp.zeros((Bz, Dz), k.dtype), jnp.zeros((Bz, Dz), k.dtype), jnp.zeros((Bz, Dz), k.dtype))

            def step(carry, kv):
                alpha, beta, eps = carry
                kt, vt = kv
                ukt = u + kt
                tau = jnp.maximum(ukt, eps)
                e1 = jnp.exp(eps - tau)
                e2 = jnp.exp(ukt - tau)
                out = (e1 * alpha + e2 * vt) / (e1 * beta + e2)
                w_eps = eps + w_log
                eps_n = jnp.maximum(w_eps, kt)
                e1n = jnp.exp(w_eps - eps_n)
                e2n = jnp.exp(kt - eps_n)
                return ((e1n * alpha + e2n * vt, e1n * beta + e2n, eps_n), out)
            _, outs = lax.scan(step, init, (jnp.swapaxes(k, 0, 1), jnp.swapaxes(v, 0, 1)))
            return jnp.swapaxes(outs, 0, 1)
        shifted = jnp.pad(hidden, ((0, 0), (1, 0), (0, 0)))[:, :-1]
        k_in = hidden * time_mix_key + shifted * (1 - time_mix_key)
        v_in = hidden * time_mix_value + shifted * (1 - time_mix_value)
        r_in = hidden * time_mix_receptance + shifted * (1 - time_mix_receptance)
        k = bit_linear(k_in, w_key, rms_key)
        v = bit_linear(v_in, w_value, rms_value)
        r = jax.nn.sigmoid(bit_linear(r_in, w_receptance, rms_receptance))
        rwkv = wkv_with_eps(time_decay, time_first, k, v)
        return bit_linear(r * rwkv, w_output, rms_output)

    def _L0_cond2_ref(hidden, W1, b1, v, prompt_type_ids):
        import jax, jax.numpy as jnp
        import numpy as np
        NEG_INF = -1e+30
        B, S, D = hidden.shape
        attn_in = jnp.tanh(jnp.einsum('bsd,da->bsa', hidden, W1) + b1)
        scores = jnp.einsum('bsa,a->bs', attn_in, v)
        idx = jnp.arange(S)
        j = idx[:, None]
        l = idx[None, :]
        prefix_m = l <= j
        postfix_m = l >= j
        cloze_m = l != j
        pt = prompt_type_ids[:, None, None]
        mask = jnp.where(pt == 0, prefix_m[None], jnp.where(pt == 1, postfix_m[None], cloze_m[None]))
        masked_scores = jnp.where(mask, scores[:, None, :], NEG_INF)
        p = jax.nn.softmax(masked_scores, axis=-1)
        cnt = jnp.sum(mask, axis=-1).astype(hidden.dtype)
        pooled = jnp.einsum('bjl,bld->bjd', p, hidden) / cnt[..., None]
        return pooled

    def _L0_ffn_ref(x, shared_gate, shared_up, shared_down, routed_gate, routed_up, routed_down, Wr, routing_bias):
        import jax, jax.numpy as jnp
        import numpy as np
        DIM = 128
        HID = 352
        N_ROUTED = 7
        TOPK = 2
        B, S = (4, 256)

        def _expert(x, wg, wu, wd):
            return jax.nn.silu(x @ wg) * (x @ wu) @ wd
        b, s, d = x.shape
        n_exp = routed_gate.shape[0]
        shared_out = _expert(x, shared_gate, shared_up, shared_down)
        logits = x @ Wr * routing_bias
        probs = jax.nn.sigmoid(logits)
        scores, idx = jax.lax.top_k(probs, TOPK)
        scores = scores / scores.sum(-1, keepdims=True)
        t = b * s
        xf = x.reshape(t, d)
        weights = jnp.zeros((t, n_exp), x.dtype).at[jnp.arange(t)[:, None], idx.reshape(t, TOPK)].add(scores.reshape(t, TOPK))
        combined = jnp.zeros_like(xf)
        for e in range(n_exp):
            combined = combined + _expert(xf, routed_gate[e], routed_up[e], routed_down[e]) * weights[:, e:e + 1]
        return shared_out + combined.reshape(b, s, d)
    x = x + _L0_attn_ref(_L0_cond_ref(x, itok_B_0_15, L0_cond_weights, L0_cond_b), L0_attn_time_decay, L0_attn_time_first, L0_attn_time_mix_key, L0_attn_time_mix_value, L0_attn_time_mix_receptance, L0_attn_w_key, L0_attn_w_value, L0_attn_w_receptance, L0_attn_w_output, L0_attn_rms_key, L0_attn_rms_value, L0_attn_rms_receptance, L0_attn_rms_output)
    x = x + _L0_ffn_ref(_L0_cond2_ref(x, L0_cond2_W1, L0_cond2_b1, L0_cond2_v, itok_B_0_2), L0_ffn_shared_gate, L0_ffn_shared_up, L0_ffn_shared_down, L0_ffn_routed_gate, L0_ffn_routed_up, L0_ffn_routed_down, L0_ffn_Wr, L0_ffn_routing_bias)
    return x

_drawn_inputs = setup_inputs


def setup_inputs(seed=0):
    import zlib

    import numpy as np

    out = dict(_drawn_inputs(seed))
    spreads = {'L0_attn_rms_key': (1.0, 0.6),
     'L0_attn_rms_value': (1.0, 0.2),
     'L0_attn_rms_receptance': (1.0, 0.6),
     'L0_attn_rms_output': (1.0, 0.2)}
    factors = {'L0_attn_time_mix_key': 2.71,
     'L0_attn_time_mix_receptance': 2.7,
     'L0_cond2_W1': 8.0,
     'L0_cond2_b1': 64.0,
     'L0_cond2_v': 8.0,
     'L0_ffn_shared_gate': 8.0,
     'L0_ffn_shared_up': 8.0,
     'L0_ffn_shared_down': 8.0,
     'L0_ffn_routed_gate': 8.0,
     'L0_ffn_routed_up': 8.0,
     'L0_ffn_routed_down': 8.0,
     'L0_ffn_Wr': 8.0,
     'L0_ffn_routing_bias': 8.0}
    for name, (base, spread) in spreads.items():
        noise = np.random.default_rng([zlib.crc32(name.encode()), seed]).standard_normal(out[name].shape)
        drawn = base * np.exp(spread * noise) if base else spread * noise
        out[name] = jnp.asarray(drawn.astype(out[name].dtype))
    for name, factor in factors.items():
        out[name] = (out[name] * factor).astype(out[name].dtype)
    return out
```

```python
from contextlib import ExitStack

import concourse.bass as bass
from concourse import mybir

ALU = mybir.AluOpType
ACT = mybir.ActivationFunctionType
AX_X = mybir.AxisListType.X
F32 = mybir.dt.float32
F32R = mybir.dt.float32r
BF16 = mybir.dt.bfloat16
I32 = mybir.dt.int32

P = 128
B, T, D = 32, 32, 128
SUBJECTS = 16
OWNER = [(0, 1, 0, 1, 2)[b % 5] for b in range(B)]
SHARE = [OWNER.count(k) for k in range(3)]
TILES = B * T // P
HALVES = 2
HB = B // HALVES
HT = TILES // HALVES
N = HB * T
TP = T + 1
HID = 352
CH = [(0, 128), (128, 128), (256, HID - 256)]
NCH = len(CH)
E_ROUTED = 7
E_ALL = E_ROUTED + 1
A_DIM = 32
GU = 2 * HID
PACK = GU + NCH * D
ROUND = 12582912.0
RMS_EPS = 1e-8
TINY = 1e-5
BIG = 1e30
COL = {n: i for i, n in enumerate(
    ["decay", "first", "mix_k", "mix_v", "mix_r", "rms_k", "rms_v", "rms_r", "rms_o"])}


def adaln_attention_ffn(nc, x, x_t, subject, prompt_type, cond, cols, attn_w, w1, b1_v,
                        router_w, router_b, experts, out):
    ctx = ExitStack()
    with ctx:
        def sb(name, shape, dt=F32):
            return ctx.enter_context(nc.sbuf_tensor(name, shape, dt))

        def sem(name):
            return ctx.enter_context(nc.semaphore(name))

        x_tok = sb("x_tok", [P, TILES, D])
        x_ch = sb("x_ch", [P, B, T])
        subj = sb("subj", [1, B], I32)
        ptype_i = sb("ptype_i", [P, TILES], I32)
        cond_w = sb("cond_w", [P, B, D + 1])
        vec = sb("vec", [P, len(COL)])
        aw = sb("aw", [P, 4, D])
        w1_sb = sb("w1_sb", [P, A_DIM])
        b1v = sb("b1v", [A_DIM, 2])
        wr = sb("wr", [P, E_ROUTED])
        rbias = sb("rbias", [P, E_ROUTED])
        raw = sb("raw", [P, 2, PACK])
        cond_all = raw[:].rearrange("p b n -> p (b n)")[:, 0:SUBJECTS * (D + 1)].rearrange(
            "p (s d) -> p s d", s=SUBJECTS)

        ident = sb("ident", [P, P])
        ones = sb("ones", [P, P])
        zeros = sb("zeros", [P, N], BF16)
        zero_col = sb("zero_col", [P, 1])
        neg_half = sb("neg_half", [P, 3 * HT])
        diff = sb("diff", [P, T])
        below = sb("below", [P, T])
        above = sb("above", [P, T])
        other = sb("other", [P, T])
        ptype = sb("ptype", [P, TILES])
        is_kind = sb("is_kind", [P, 3, TILES])
        mask = sb("mask", [P, TILES, T])
        mask_b = sb("mask_b", [P, TILES, T])
        penalty = sb("penalty", [P, TILES, T])
        count = sb("count", [P, TILES])
        rank = sb("rank", [P, E_ROUTED])
        one_less = sb("one_less", [P, 3])
        decay = sb("decay", [P, 1])
        log_w = sb("log_w", [P, 1])
        scan_w = sb("scan_w", [P, HB, TP])

        abs_sum = sb("abs_sum", [P, 4])
        w_mean = sb("w_mean", [P, 4])
        w_scale = sb("w_scale", [P, 4])
        w_back = sb("w_back", [P, 4])
        w_round = sb("w_round", [P, 4, D])
        w_clip = sb("w_clip", [P, 4, D])
        w_q = sb("w_q", [P, 4, D], BF16)

        h_pad = sb("h_pad", [P, HALVES, HB, TP])
        shifted = sb("shifted", [P, HALVES, 3, N])
        mixed = sb("mixed", [P, HALVES, 3, N])
        square = sb("square", [P, HALVES, 3, N])
        weighted = sb("weighted", [P, HALVES, 3, N])
        scaled = mixed
        quant = sb("quant", [P, HALVES, 3, N], BF16)
        stat = sb("stat", [P, HALVES, 8, 3 * HT])
        back = square
        k_pad = sb("k_pad", [P, HALVES, HB, TP])
        val, rec, exp_r = (shifted[:, :, m, :] for m in range(3))
        eps = sb("eps", [P, HALVES, HB, TP])
        dec_arg, new_arg = weighted[:, :, 1, :], weighted[:, :, 2, :]
        dec_pad = sb("dec_pad", [P, HALVES, HB, TP])
        new_pad = sb("new_pad", [P, HALVES, HB, TP])
        newv_pad = sb("newv_pad", [P, HALVES, HB, TP])
        alpha = sb("alpha", [P, HALVES, HB, TP])
        beta = sb("beta", [P, HALVES, HB, TP])
        tau, arg = mixed[:, :, 0, :], mixed[:, :, 1:3, :]
        e12 = sb("e12", [P, HALVES, 2, N])
        prod = cond_w[:].rearrange("p b d -> p (b d)")[:, 0:HALVES * 4 * N].rearrange(
            "p (h k n) -> p h k n", h=HALVES, k=4)
        mixed_o = weighted[:, :, 2, :]
        x2 = sb("x2", [P, TILES, D])
        x2_t = weighted[:, :, 1, :]
        tanh_t = sb("tanh_t", [A_DIM, HALVES, N])
        scores = sb("scores", [P, HALVES, HT, T])
        soft = sb("soft", [P, HALVES, HT, T])
        soft_n = sb("soft_n", [P, HALVES, HT, T])
        row = sb("row", [P, HALVES, 4, HT])
        blocks = sb("blocks", [P, HALVES, HT, P])
        y = x_ch[:].rearrange("p (h b) t -> p h (b t)", h=HALVES)
        y_hi = sb("y_hi", [P, HALVES, N], F32R)
        y_lo = sb("y_lo", [P, HALVES, N], F32R)
        gate_e = sb("gate_e", [P, HALVES, 8, HT, E_ROUTED])
        gate_t = sb("gate_t", [P, HALVES, 8, HT])
        route = sb("route", [P, HALVES, HT, E_ALL])
        route_col = sb("route_col", [P, HALVES, HT])

        w_hi = [sb(f"w_hi{i}", [P, PACK], F32R) for i in range(2)]
        w_lo = [sb(f"w_lo{i}", [P, PACK], F32R) for i in range(2)]
        yw = mixed[:, 0, 2, :]
        yw_hi = [sb(f"yw_hi{i}", [P, N], F32R) for i in range(2)]
        yw_lo = [sb(f"yw_lo{i}", [P, N], F32R) for i in range(2)]
        silu, hid = mixed[:, 0, 0:2, :], mixed[:, 1, 0:2, :]
        hid_hi = [sb(f"hid_hi{i}", [P, N], F32R) for i in range(NCH)]
        hid_lo = [sb(f"hid_lo{i}", [P, N], F32R) for i in range(NCH)]
        acc_sb = square[:, :, 0, :]
        final = weighted[:].rearrange("p h m n -> p (h m n)")[:, 0:TILES * D].rearrange(
            "p (n d) -> p n d", n=TILES)

        ps = [ctx.enter_context(nc.psum_tensor(f"ps{i}", [P, 512], F32)) for i in range(8)]
        gate_ps, up_ps, bc_ps, acc_ps = ps[0:2], ps[2:4], ps[4:6], ps[6:8]

        def tiles(ap):
            return ap.rearrange("p (n c) -> p n c", n=HT)

        def steps(ap):
            return ap.rearrange("p (b t) -> p b t", t=T)

        def lane(ap, n):
            return ap.broadcast_to([P, n])

        names = """in_subj in_xt in_vec in_aw in_small in_x in_type in_cond stored
            const_ready zero_ready ident_ready one_less_done decay_done log_w_ready scan_ready abs_ready
            tot_ready w_q_ready back_ready penalty_ready count_ready ptype_ready
            h_ps h_ready shift_ready mix_ready square_ready weighted_ready weighted_t sumsq_ready
            meansq_ready rms_ready scale_ready scale_bc quant_ready proj_ready back_bc back_sb
            k_ready r_ready exp_r_ready dec_arg_ready new_arg_ready dec_ready new_ready
            arg_ready e12_ready o_ready sq_o wo_ready wo_t sumsq_o meansq_o rms_o scale_o
            bc_o quant_o out_ps x2_ready x2_t_ps x2_t_ready w1_ps tanh_ready score_ps
            soft_arg exp_s blocks_ready pooled_ps y_ready y_hi_ready y_split logit_ps logit_ready
            exp_l route_ready vec_step pool_step pool_in
            weight_split column_ready expert_used bc_ready yw_ready yw_hi_ready yw_split gu_ready silu_ready
            hid_ready hid_hi_ready hid_split acc_ready acc_out out_t out_ready""".split()
        s = {n: sem(n) for n in names}

        gathered = [sem(f"gathered_{n}") for n in ("vector", "scalar", "gpsimd")]

        def gather(eng, k, copy):
            eng.wait_ge(s["in_subj"], 16)
            mine = [b for b in range(B) if OWNER[b] == k]
            who = [eng.value_load(subj[0:1, b:b + 1], min_val=0, max_val=SUBJECTS - 1) for b in mine]
            eng.wait_ge(s["in_cond"], 16)
            for b, r in zip(mine, who):
                copy(cond_w[:, b:b + 1, :], cond_all[:, bass.ds(r, 1), :]).then_inc(gathered[k], 1)

        expert_in = [sem(f"expert_in{b}") for b in range(2)]

        block = ctx.enter_context(nc.Block())

        @block.sync
        def _(sp):
            sp.dma_start(subj[:], subject).then_inc(s["in_subj"], 16)
            sp.dma_start(x_ch[:].rearrange("p b t -> p (b t)"), x_t).then_inc(s["in_xt"], 16)
            sp.dma_start(cond_all[:].rearrange("p s d -> p (s d)"), cond).then_inc(s["in_cond"], 16)
            for k in range(3):
                sp.wait_ge(gathered[k], SHARE[k])
            for e in range(2):
                sp.dma_start(raw[:, e, :], experts[e]).then_inc(expert_in[e], 16)
            with sp.Fori(0, E_ALL // 2 - 1) as i:
                for b in range(2):
                    sp.wait_ge(s["weight_split"], i * 2 + (b + 1))
                    sp.dma_start(raw[:, b, :], experts[bass.ds(i * 2 + (b + 2), 1)].rearrange(
                        "e p n -> p (e n)")).then_inc(expert_in[b], 16)
            sp.wait_ge(s["out_ready"], 1)
            o_v = out.rearrange("b t d -> (b t) d").rearrange("(n p) d -> p n d", p=P)
            sp.dma_start(o_v[:, 0:HT, :], final[:, 0:HT, :]).then_inc(s["stored"], 16)
            sp.wait_ge(s["out_ready"], 2)
            sp.dma_start(o_v[:, HT:, :], final[:, HT:, :]).then_inc(s["stored"], 16)
            sp.wait_ge(s["stored"], 32)

        @block.gpsimd
        def _(pool):
            step = [0]

            def then(ins):
                step[0] += 1
                ins.then_inc(s["pool_step"], 1)
                pool.wait_ge(s["pool_step"], step[0])

            pool.memset(ident[:], 0.0).then_inc(s["zero_ready"], 1)
            pool.wait_ge(s["zero_ready"], 1)
            pool.affine_select(out=ident[:], in_=ident[:], compare_op=ALU.not_equal, fill=1.0, base=0,
                               pattern=[[-1, P]], channel_multiplier=1).then_inc(s["ident_ready"], 1)
            pool.memset(ones[:], 1.0).then_inc(s["const_ready"], 1)
            pool.memset(zero_col[:], 0.0).then_inc(s["const_ready"], 1)
            pool.memset(neg_half[:], -0.5).then_inc(s["const_ready"], 1)
            pool.memset(h_pad[:, :, :, 0:1], 0.0).then_inc(s["const_ready"], 1)
            pool.memset(k_pad[:, :, :, 0:1], 0.0).then_inc(s["const_ready"], 1)
            pool.memset(dec_pad[:, :, :, 0:1], 0.0).then_inc(s["const_ready"], 1)
            pool.memset(new_pad[:, :, :, 0:1], 0.0).then_inc(s["const_ready"], 1)
            pool.memset(newv_pad[:, :, :, 0:1], 0.0).then_inc(s["const_ready"], 1)
            pool.memset(zeros[:], 0.0).then_inc(s["const_ready"], 1)
            pool.memset(blocks[:], 0.0).then_inc(s["const_ready"], 1)
            pool.memset(route[:], 1.0).then_inc(s["const_ready"], 1)
            gather(pool, 2, pool.tensor_copy)
            pool.wait_ge(s["const_ready"], 11)
            for g in range(4):
                then(pool.iota(diff[32 * g:32 * g + 32, :], pattern=[[1, T]], base=0,
                               channel_multiplier=-1, allow_small_or_imprecise_dtypes=True))
            then(pool.iota(rank[:], pattern=[[-1, E_ROUTED]], base=E_ROUTED, channel_multiplier=0,
                           allow_small_or_imprecise_dtypes=True))
            then(pool.tensor_scalar(below[:], diff[:], 0.0, None, ALU.is_le))
            then(pool.tensor_scalar(above[:], diff[:], 0.0, None, ALU.is_ge))
            then(pool.tensor_tensor(other[:], below[:], above[:], ALU.add))
            then(pool.tensor_scalar(other[:], other[:], -1.0, 2.0, ALU.mult, ALU.add))
            pool.wait_ge(s["in_type"], 64)
            then(pool.tensor_copy(ptype[:], ptype_i[:]))
            then(pool.tensor_scalar(is_kind[:, 0, :], ptype[:], 0.0, None, ALU.is_equal))
            then(pool.tensor_scalar(is_kind[:, 1, :], ptype[:], 1.0, None, ALU.is_equal))
            then(pool.tensor_tensor(is_kind[:, 2, :], is_kind[:, 0, :], is_kind[:, 1, :], ALU.add))
            then(pool.tensor_scalar(is_kind[:, 2, :], is_kind[:, 2, :], -1.0, 1.0, ALU.mult, ALU.add))
            shape = [P, TILES, T]

            def term(dst, kind, rows):
                then(pool.tensor_tensor(dst[:], is_kind[:, kind, :].unsqueeze(2).broadcast_to(shape),
                                        rows[:].unsqueeze(1).broadcast_to(shape), ALU.mult))
            term(mask, 0, below)
            term(mask_b, 1, above)
            then(pool.tensor_tensor(mask[:], mask[:], mask_b[:], ALU.add))
            term(mask_b, 2, other)
            then(pool.tensor_tensor(mask[:], mask[:], mask_b[:], ALU.add))
            pool.tensor_scalar(penalty[:], mask[:], BIG, -BIG, ALU.mult, ALU.add
                               ).then_inc(s["penalty_ready"], 1)
            for half in range(HALVES):
                pool.wait_ge(s["meansq_ready"], half + 1)
                pool.tensor_tensor(stat[:, half, 1, :], stat[:, half, 0, :], neg_half[:], ALU.pow
                                   ).then_inc(s["rms_ready"], 1)
            for half in range(HALVES):
                pool.wait_ge(s["meansq_o"], half + 1)
                pool.tensor_tensor(stat[:, half, 1, 0:HT], stat[:, half, 0, 0:HT], neg_half[:, 0:HT],
                                   ALU.pow).then_inc(s["rms_o"], 1)

            def split(e, pair, b):
                w = raw[:, b, :]
                pool.wait_ge(expert_in[b], (pair + 1) * 16)
                pool.tensor_tensor(w_hi[b][:], w, zero_col[:].broadcast_to([P, PACK]), ALU.add).then_inc(s["pool_in"], 1)
                pool.wait_ge(s["pool_in"], e + 1)
                pool.tensor_tensor(w_lo[b][:], w, w_hi[b][:].bitcast(F32), ALU.subtract
                                   ).then_inc(s["weight_split"], 1)
            split(0, 0, 0)
            split(1, 0, 1)
            with pool.Fori(0, E_ALL // 2 - 1) as i:
                for b in range(2):
                    pool.wait_ge(s["expert_used"], i * 2 + (b + 1))
                    split(i * 2 + (b + 2), i + 1, b)

        @block.scalar
        def _(act):
            act.dma_start(vec[:], cols).then_inc(s["in_vec"], 16)
            act.dma_start(aw[:].rearrange("p m d -> p (m d)"), attn_w).then_inc(s["in_aw"], 16)
            act.dma_start(x_tok[:], x.rearrange("b t d -> (b t) d").rearrange("(n p) d -> p n d", p=P)
                          ).then_inc(s["in_x"], 16)
            for g in range(4):
                act.dma_start(ptype_i[32 * g:32 * g + 32, :],
                              prompt_type[g:g + 1, :].broadcast_to([32, TILES])
                              ).then_inc(s["in_type"], 16)
            act.dma_start(w1_sb[:], w1).then_inc(s["in_small"], 16)
            act.dma_start(b1v[:], b1_v).then_inc(s["in_small"], 16)
            act.dma_start(wr[:], router_w).then_inc(s["in_small"], 16)
            act.dma_start(rbias[:], router_b.broadcast_to([P, E_ROUTED])).then_inc(s["in_small"], 16)
            gather(act, 1, lambda o, x: act.activation(o, x, ACT.Copy))
            act.wait_ge(s["in_vec"], 16)
            act.activation(decay[:], vec[:, 0:1], ACT.Exp).then_inc(s["decay_done"], 1)

            def per_half(f):
                for half in range(HALVES):
                    f(half)

            def shift(half):
                act.wait_ge(s["h_ready"], half + 1)
                act.wait_ge(s["one_less_done"], 1)
                for m in range(3):
                    act.activation(steps(shifted[:, half, m, :]), h_pad[:, half, :, 0:T], ACT.Identity,
                                   scale=one_less[:, m:m + 1]).then_inc(s["shift_ready"], 1)
            per_half(shift)

            def squares(half):
                for m in range(3):
                    act.wait_ge(s["mix_ready"], 3 * half + m + 1)
                    act.activation(square[:, half, m, :], mixed[:, half, m, :], ACT.Square
                                   ).then_inc(s["square_ready"], 1)
            per_half(squares)

            def backs(half):
                for m in range(3):
                    act.wait_ge(s["back_bc"], 3 * half + m + 1)
                    act.activation(back[:, half, m, :], ps[4 * half][:], ACT.Copy
                                   ).then_inc(s["back_sb"], 1)
            per_half(backs)

            def exps(half):
                act.wait_ge(s["dec_arg_ready"], half + 1)
                act.activation(dec_pad[:, half, :, 1:TP], steps(dec_arg[:, half, :]), ACT.Exp,
                               bias=log_w[:, 0:1]).then_inc(s["dec_ready"], 1)
                act.wait_ge(s["new_arg_ready"], half + 1)
                act.activation(new_pad[:, half, :, 1:TP], steps(new_arg[:, half, :]), ACT.Exp
                               ).then_inc(s["new_ready"], 1)
                for j in range(2):
                    act.wait_ge(s["arg_ready"], 2 * half + j + 1)
                    act.activation(e12[:, half, j, :], arg[:, half, j, :], ACT.Exp
                                   ).then_inc(s["e12_ready"], 1)
                act.wait_ge(s["r_ready"], half + 1)
                act.activation(exp_r[:, half, :], rec[:, half, :], ACT.Exp, scale=-1.0
                               ).then_inc(s["exp_r_ready"], 1)
            per_half(exps)

            def square_o(half):
                act.wait_ge(s["o_ready"], half + 1)
                act.activation(square[:, half, 0, :], mixed_o[:, half, :], ACT.Square
                               ).then_inc(s["sq_o"], 1)
            per_half(square_o)

            def pool_in(half):
                act.wait_ge(s["x2_t_ps"], half + 1)
                act.activation(x2_t[:, half, :], ps[4 * half + 1][:], ACT.Copy
                               ).then_inc(s["x2_t_ready"], 1)
                act.wait_ge(s["w1_ps"], half + 1)
                act.wait_ge(s["in_small"], 64)
                act.activation(tanh_t[:, half, :], ps[4 * half + 2][0:A_DIM, :], ACT.Tanh,
                               bias=b1v[:, 0:1]).then_inc(s["tanh_ready"], 1)
            per_half(pool_in)

            def softmax(half):
                act.wait_ge(s["soft_arg"], half + 1)
                act.activation(soft[:, half], scores[:, half], ACT.Exp).then_inc(s["exp_s"], 1)
            per_half(softmax)

            def y_copy(half):
                act.wait_ge(s["pooled_ps"], half + 1)
                act.activation(y[:, half, :], ps[4 * half + 1][:], ACT.Copy).then_inc(s["y_ready"], 1)
                act.activation(y_hi[:, half, :], ps[4 * half + 1][:], ACT.Copy
                               ).then_inc(s["y_hi_ready"], 1)
            per_half(y_copy)

            def route_exp(half):
                act.wait_ge(s["logit_ready"], half + 1)
                act.activation(gate_e[:, half, 1], gate_e[:, half, 0], ACT.Exp, scale=-1.0
                               ).then_inc(s["exp_l"], 1)
            per_half(route_exp)

            def yw_high(n, b):
                act.wait_ge(s["yw_ready"], n + 1)
                act.activation(yw_hi[b][:], yw, ACT.Copy).then_inc(s["yw_hi_ready"], 1)

            def chunk(q, b, c):
                rows = CH[c][1]
                act.wait_ge(s["gu_ready"], q + 1)
                act.activation(silu[0:rows, b, :], gate_ps[b][0:rows, :], ACT.Silu
                               ).then_inc(s["silu_ready"], 1)

            def high(q, b, c):
                rows = CH[c][1]
                act.wait_ge(s["hid_ready"], q + 1)
                act.activation(hid_hi[c][0:rows, :], hid[0:rows, b, :], ACT.Copy
                               ).then_inc(s["hid_hi_ready"], 1)

            yw_high(0, 0)
            yw_high(1, 1)
            for c in range(NCH):
                chunk(c, c % 2, c)
                if c:
                    high(c - 1, (c - 1) % 2, c - 1)

            def body(i, last):
                for u in range(4):
                    for c in range(NCH):
                        k = NCH * u + c
                        if not (last and u == 3):
                            chunk(i * (4 * NCH) + (k + 3), (k + 3) % 2, c)
                        if last and u == 3 and c == 0:
                            act.wait_ge(s["acc_ready"], 1)
                        if not (last and u == 3 and c > 0):
                            high(i * (4 * NCH) + (k + 2), k % 2, (c + 2) % NCH)
                        if c == 0 and not (last and u >= 2):
                            yw_high(i * 4 + (u + 2), u % 2)

            with act.Fori(0, E_ALL // 2 - 1) as i:
                body(i, False)
            body(E_ALL // 2 - 1, True)
            for half in range(HALVES):
                act.wait_ge(*((s["acc_ready"], 1) if half == 0 else (s["expert_used"], E_ALL)))
                act.activation(acc_sb[:, half, :], acc_ps[half][:], ACT.Copy).then_inc(s["acc_out"], 1)

        @block.vector
        def _(v):
            step = [0]

            def then(ins):
                step[0] += 1
                ins.then_inc(s["vec_step"], 1)
                v.wait_ge(s["vec_step"], step[0])

            gather(v, 0, v.tensor_copy)
            v.wait_ge(s["in_vec"], 16)
            v.tensor_scalar(one_less[:], vec[:, 2:5], -1.0, 1.0, ALU.mult, ALU.add
                            ).then_inc(s["one_less_done"], 1)
            v.wait_ge(s["in_aw"], 16)
            v.tensor_reduce(abs_sum[:], aw[:], AX_X, ALU.add, apply_absolute_value=True
                            ).then_inc(s["abs_ready"], 1)
            v.wait_ge(s["decay_done"], 1)
            v.tensor_scalar(log_w[:], decay[:], -1.0, None, ALU.mult).then_inc(s["log_w_ready"], 1)
            v.wait_ge(s["log_w_ready"], 1)
            v.wait_ge(s["const_ready"], 11)
            then(v.tensor_scalar(scan_w[:, :, 1:TP], h_pad[:, 0, :, 0:1].broadcast_to([P, HB, T]),
                                 log_w[:, 0:1], None, ALU.add))
            v.memset(scan_w[:, :, 0:1], -BIG).then_inc(s["scan_ready"], 1)
            v.wait_ge(s["tot_ready"], 1)
            then(v.tensor_scalar(w_mean[:], ps[7][:, 0:4], 1.0 / (D * D), TINY, ALU.mult, ALU.max))
            then(v.reciprocal(w_scale[:], w_mean[:]))
            v.tensor_scalar(w_back[:], w_mean[:], 1.0 / 127.0, None, ALU.mult).then_inc(s["back_ready"], 1)
            for m in range(4):
                last = v.tensor_scalar(w_round[:, m, :], aw[:, m, :], w_scale[:, m:m + 1], ROUND,
                                       ALU.mult, ALU.add)
            then(last)
            then(v.tensor_scalar(w_clip[:], w_round[:], -ROUND, 1.0, ALU.add, ALU.min))
            v.tensor_scalar(w_q[:], w_clip[:], -1.0, None, ALU.max).then_inc(s["w_q_ready"], 1)

            def per_half(f):
                for half in range(HALVES):
                    f(half)

            def h_out(half):
                v.wait_ge(s["h_ps"], half + 1)
                v.tensor_tensor(h_pad[:, half, :, 1:TP], steps(ps[4 * half][:]),
                                cond_w[:, half * HB:(half + 1) * HB, D:D + 1].broadcast_to([P, HB, T]),
                                ALU.add).then_inc(s["h_ready"], 1)
            per_half(h_out)

            def mix(half):
                v.wait_ge(s["h_ready"], half + 1)
                for m in range(3):
                    v.wait_ge(s["shift_ready"], 3 * half + m + 1)
                    v.scalar_tensor_tensor(out=steps(mixed[:, half, m, :]), in0=h_pad[:, half, :, 1:TP],
                                           scalar=vec[:, 2 + m:3 + m], in1=steps(shifted[:, half, m, :]),
                                           op0=ALU.mult, op1=ALU.add).then_inc(s["mix_ready"], 1)
                for m in range(3):
                    v.wait_ge(s["mix_ready"], 3 * half + m + 1)
                    v.tensor_scalar(weighted[:, half, m, :], mixed[:, half, m, :], vec[:, 5 + m:6 + m],
                                    None, ALU.mult).then_inc(s["weighted_ready"], 1)
            per_half(mix)

            def scale_rows(half, n, peak_from, sumsq, rms_sem, meansq_sem, back_w, done):
                st = stat[:, half]
                peak_from()
                v.wait_ge(sumsq[0], half + 1)
                v.tensor_scalar(st[:, 0, 0:n], sumsq[1], 1.0 / D, RMS_EPS, ALU.mult, ALU.add
                                ).then_inc(meansq_sem, 1)
                v.wait_ge(rms_sem, half + 1)
                then(v.tensor_tensor(st[:, 3, 0:n], st[:, 2, 0:n], st[:, 1, 0:n], ALU.mult))
                then(v.tensor_scalar(st[:, 4, 0:n], st[:, 3, 0:n], TINY, None, ALU.max))
                then(v.reciprocal(st[:, 5, 0:n], st[:, 4, 0:n]))
                v.scalar_tensor_tensor(out=st[:, 6, 0:n], in0=st[:, 1, 0:n], scalar=127.0,
                                       in1=st[:, 5, 0:n], op0=ALU.mult, op1=ALU.mult).then_inc(done, 1)
                v.tensor_tensor(st[:, 7, 0:n].rearrange("p (m n) -> p m n", n=HT),
                                st[:, 4, 0:n].rearrange("p (m n) -> p m n", n=HT), back_w,
                                ALU.mult).then_inc(done, 1)

            def scales(half):
                def peaks():
                    for m in range(3):
                        v.wait_ge(s["weighted_t"], 3 * half + m + 1)
                        last = v.tensor_reduce(stat[:, half, 2, HT * m:HT * m + HT],
                                               tiles(ps[4 * half + 1 + m][:]), AX_X, ALU.max,
                                               apply_absolute_value=True)
                    then(last)
                v.wait_ge(s["back_ready"], 1)
                scale_rows(half, 3 * HT, peaks, (s["sumsq_ready"], ps[4 * half][:, 0:3 * HT]),
                           s["rms_ready"], s["meansq_ready"],
                           w_back[:, 0:3].unsqueeze(2).broadcast_to([P, 3, HT]), s["scale_ready"])
            per_half(scales)

            def quantise(half):
                for m in range(3):
                    v.wait_ge(s["scale_bc"], 3 * half + m + 1)
                    v.wait_ge(s["weighted_ready"], 3 * half + m + 1)
                    then(v.tensor_tensor(scaled[:, half, m, :], weighted[:, half, m, :],
                                         ps[4 * half + 1 + m][:], ALU.mult))
                    v.tensor_scalar(quant[:, half, m, :], scaled[:, half, m, :], ROUND, -ROUND,
                                    ALU.add, ALU.add).then_inc(s["quant_ready"], 1)
            per_half(quantise)

            def wkv_args(half):
                v.wait_ge(s["proj_ready"], 3 * half + 1)
                v.wait_ge(s["back_sb"], 3 * half + 1)
                v.tensor_tensor(k_pad[:, half, :, 1:TP], steps(ps[4 * half + 1][:]),
                                steps(back[:, half, 0, :]), ALU.mult).then_inc(s["k_ready"], 1)
                v.wait_ge(s["k_ready"], half + 1)
                v.wait_ge(s["scan_ready"], 1)
                flat = "p b t -> p (b t)"
                then(v.tensor_tensor_scan(eps[:, half].rearrange(flat), scan_w[:].rearrange(flat),
                                          k_pad[:, half].rearrange(flat), 0.0, ALU.add, ALU.max))
                old, new, k = eps[:, half, :, 0:T], eps[:, half, :, 1:TP], k_pad[:, half, :, 1:TP]
                v.tensor_tensor(steps(dec_arg[:, half, :]), old, new, ALU.subtract
                                ).then_inc(s["dec_arg_ready"], 1)
                v.tensor_tensor(steps(new_arg[:, half, :]), k, new, ALU.subtract
                                ).then_inc(s["new_arg_ready"], 1)
                then(v.scalar_tensor_tensor(out=steps(tau[:, half, :]), in0=k, scalar=vec[:, 1:2],
                                            in1=old, op0=ALU.add, op1=ALU.max))
                v.tensor_tensor(steps(arg[:, half, 0, :]), old, steps(tau[:, half, :]), ALU.subtract
                                ).then_inc(s["arg_ready"], 1)
                v.scalar_tensor_tensor(out=steps(arg[:, half, 1, :]), in0=k, scalar=vec[:, 1:2],
                                       in1=steps(tau[:, half, :]), op0=ALU.add, op1=ALU.subtract
                                       ).then_inc(s["arg_ready"], 1)
                v.wait_ge(s["proj_ready"], 3 * half + 3)
                v.wait_ge(s["back_sb"], 3 * half + 3)
                v.tensor_tensor(rec[:, half, :], ps[4 * half + 3][:], back[:, half, 2, :], ALU.mult
                                ).then_inc(s["r_ready"], 1)
                then(v.tensor_tensor(val[:, half, :], ps[4 * half + 2][:], back[:, half, 1, :], ALU.mult))
            per_half(wkv_args)

            def wkv(half):
                flat = "p b t -> p (b t)"
                v.wait_ge(s["new_ready"], half + 1)
                v.wait_ge(s["dec_ready"], half + 1)
                then(v.tensor_tensor(newv_pad[:, half, :, 1:TP], new_pad[:, half, :, 1:TP],
                                     steps(val[:, half, :]), ALU.mult))
                v.tensor_tensor_scan(beta[:, half].rearrange(flat), dec_pad[:, half].rearrange(flat),
                                     new_pad[:, half].rearrange(flat), 0.0, ALU.mult, ALU.add)
                then(v.tensor_tensor_scan(alpha[:, half].rearrange(flat), dec_pad[:, half].rearrange(flat),
                                          newv_pad[:, half].rearrange(flat), 0.0, ALU.mult, ALU.add))
                v.wait_ge(s["e12_ready"], 2 * half + 2)
                pr = prod[:, half]
                e1, e2 = e12[:, half, 0, :], e12[:, half, 1, :]
                v.tensor_tensor(steps(pr[:, 0, :]), steps(e1), beta[:, half, :, 0:T], ALU.mult)
                v.tensor_tensor(steps(pr[:, 1, :]), steps(e1), alpha[:, half, :, 0:T], ALU.mult)
                then(v.tensor_tensor(pr[:, 2, :], e2, val[:, half, :], ALU.mult))
                then(v.tensor_tensor(pr[:, 0, :], pr[:, 0, :], e2, ALU.add))
                v.wait_ge(s["exp_r_ready"], half + 1)
                then(v.scalar_tensor_tensor(out=pr[:, 3, :], in0=exp_r[:, half, :], scalar=1.0,
                                            in1=pr[:, 0, :], op0=ALU.add, op1=ALU.mult))
                v.reciprocal(pr[:, 0, :], pr[:, 3, :])
                then(v.tensor_tensor(pr[:, 1, :], pr[:, 1, :], pr[:, 2, :], ALU.add))
                v.tensor_tensor(mixed_o[:, half, :], pr[:, 1, :], pr[:, 0, :], ALU.mult
                                ).then_inc(s["o_ready"], 1)
                v.wait_ge(s["o_ready"], half + 1)
                v.tensor_scalar(weighted[:, half, 0, :], mixed_o[:, half, :], vec[:, 8:9], None, ALU.mult
                                ).then_inc(s["wo_ready"], 1)
            per_half(wkv)

            def scales_o(half):
                def peaks():
                    v.wait_ge(s["wo_t"], half + 1)
                    then(v.tensor_reduce(stat[:, half, 2, 0:HT], tiles(ps[4 * half + 1][:]), AX_X,
                                         ALU.max, apply_absolute_value=True))
                scale_rows(half, HT, peaks, (s["sumsq_o"], ps[4 * half][:, 0:HT]), s["rms_o"],
                           s["meansq_o"], w_back[:, 3:4].unsqueeze(2).broadcast_to([P, 1, HT]),
                           s["scale_o"])
            per_half(scales_o)

            def quantise_o(half):
                v.wait_ge(s["bc_o"], half + 1)
                then(v.tensor_tensor(scaled[:, half, 0, :], weighted[:, half, 0, :],
                                     ps[4 * half + 2][:], ALU.mult))
                v.tensor_scalar(quant[:, half, 0, :], scaled[:, half, 0, :], ROUND, -ROUND,
                                ALU.add, ALU.add).then_inc(s["quant_o"], 1)
            per_half(quantise_o)

            def residual(half):
                v.wait_ge(s["out_ps"], half + 1)
                v.wait_ge(s["in_x"], 16)
                for n in range(HT):
                    t = half * HT + n
                    last = v.scalar_tensor_tensor(out=x2[:, t, :], in0=ps[4 * half + 3][:, n * D:(n + 1) * D],
                                                  scalar=stat[:, half, 7, n:n + 1], in1=x_tok[:, t, :],
                                                  op0=ALU.mult, op1=ALU.add)
                last.then_inc(s["x2_ready"], 1)
            per_half(residual)
            v.wait_ge(s["penalty_ready"], 1)
            v.tensor_reduce(count[:], mask[:], AX_X, ALU.add).then_inc(s["count_ready"], 1)

            def soft_in(half):
                v.wait_ge(s["score_ps"], half + 1)
                for g in range(4):
                    r = slice(32 * g, 32 * g + 32)
                    last = v.tensor_tensor(scores[r, half], tiles(ps[4 * half][:])[r, :, 32 * g:32 * g + 32],
                                           penalty[r, half * HT:(half + 1) * HT, :], ALU.add)
                then(last)
                then(v.tensor_reduce(row[:, half, 0, :], scores[:, half], AX_X, ALU.max))
                v.tensor_tensor(scores[:, half], scores[:, half],
                                row[:, half, 0, :].unsqueeze(2).broadcast_to([P, HT, T]), ALU.subtract
                                ).then_inc(s["soft_arg"], 1)
            per_half(soft_in)

            def soft_out(half):
                v.wait_ge(s["exp_s"], half + 1)
                v.wait_ge(s["count_ready"], 1)
                then(v.tensor_reduce(row[:, half, 1, :], soft[:, half], AX_X, ALU.add))
                then(v.tensor_tensor(row[:, half, 2, :], row[:, half, 1, :],
                                     count[:, half * HT:(half + 1) * HT], ALU.mult))
                then(v.reciprocal(row[:, half, 3, :], row[:, half, 2, :]))
                then(v.tensor_tensor(soft_n[:, half], soft[:, half],
                                     row[:, half, 3, :].unsqueeze(2).broadcast_to([P, HT, T]), ALU.mult))
                for g in range(4):
                    r = slice(32 * g, 32 * g + 32)
                    last = v.transpose(blocks[r, half, :, 32 * g:32 * g + 32], soft_n[r, half])
                last.then_inc(s["blocks_ready"], 1)
            per_half(soft_out)

            def router(half):
                v.wait_ge(s["y_hi_ready"], half + 1)
                v.tensor_tensor(y_lo[:, half, :], y[:, half, :], y_hi[:, half, :].bitcast(F32),
                                ALU.subtract).then_inc(s["y_split"], 1)
                wide = [P, HT, E_ROUTED]
                ge, gt = gate_e[:, half], gate_t[:, half]

                def over(k):
                    return gt[:, k, :].unsqueeze(2).broadcast_to(wide)
                rk = rank[:].unsqueeze(1).broadcast_to(wide)
                v.wait_ge(s["logit_ps"], half + 1)
                v.tensor_tensor(ge[:, 0], ps[4 * half + 2][:, 0:HT * E_ROUTED].rearrange(
                    "p (n e) -> p n e", n=HT), rbias[:].unsqueeze(1).broadcast_to(wide), ALU.mult
                                ).then_inc(s["logit_ready"], 1)
                v.wait_ge(s["exp_l"], half + 1)
                then(v.tensor_scalar(ge[:, 2], ge[:, 1], 1.0, None, ALU.add))
                then(v.reciprocal(ge[:, 3], ge[:, 2]))
                for k, probs in ((0, 3), (1, 6)):
                    then(v.tensor_reduce(gt[:, k, :], ge[:, probs], AX_X, ALU.max))
                    then(v.tensor_tensor(ge[:, 4], ge[:, probs], over(k), ALU.is_equal))
                    then(v.tensor_tensor(ge[:, 4], ge[:, 4], rk, ALU.mult))
                    then(v.tensor_reduce(gt[:, 2 + k, :], ge[:, 4], AX_X, ALU.max))
                    then(v.tensor_tensor(ge[:, 5 + 2 * k], rk, over(2 + k), ALU.is_equal))
                    if k == 0:
                        then(v.scalar_tensor_tensor(out=ge[:, 6], in0=ge[:, 5], scalar=-2.0,
                                                    in1=ge[:, 3], op0=ALU.mult, op1=ALU.add))
                then(v.tensor_tensor(gt[:, 4, :], gt[:, 0, :], gt[:, 1, :], ALU.add))
                then(v.reciprocal(gt[:, 5, :], gt[:, 4, :]))
                v.tensor_tensor(gt[:, 6, :], gt[:, 0, :], gt[:, 5, :], ALU.mult)
                then(v.tensor_tensor(gt[:, 7, :], gt[:, 1, :], gt[:, 5, :], ALU.mult))
                v.tensor_tensor(ge[:, 5], ge[:, 5], over(6), ALU.mult)
                then(v.tensor_tensor(ge[:, 7], ge[:, 7], over(7), ALU.mult))
                v.tensor_tensor(route[:, half, :, 0:E_ROUTED], ge[:, 5], ge[:, 7], ALU.add
                                ).then_inc(s["route_ready"], 1)
            per_half(router)

            def yw_product(n, b):
                v.wait_ge(s["bc_ready"], n + 1)
                if not isinstance(n, int) or n:
                    v.wait_ge(s["yw_split"], n)
                v.tensor_tensor(yw, y[:, b, :], bc_ps[b][:], ALU.mult).then_inc(s["yw_ready"], 1)

            def yw_low(n, b):
                v.wait_ge(s["yw_hi_ready"], n + 1)
                v.tensor_tensor(yw_lo[b][:], yw, yw_hi[b][:].bitcast(F32), ALU.subtract
                                ).then_inc(s["yw_split"], 1)

            def product(q, b, c):
                rows = CH[c][1]
                v.wait_ge(s["silu_ready"], q + 1)
                if not isinstance(q, int) or q > 1:
                    v.wait_ge(s["hid_split"], q - 1)
                v.tensor_tensor(hid[0:rows, b, :], silu[0:rows, b, :], up_ps[b][0:rows, :], ALU.mult
                                ).then_inc(s["hid_ready"], 1)

            def low(q, b, c):
                rows = CH[c][1]
                v.wait_ge(s["hid_hi_ready"], q + 1)
                v.tensor_tensor(hid_lo[c][0:rows, :], hid[0:rows, b, :],
                                hid_hi[c][0:rows, :].bitcast(F32), ALU.subtract
                                ).then_inc(s["hid_split"], 1)

            def column(e, half):
                v.tensor_copy(route_col[:, half, :].unsqueeze(2),
                              route[:, half, :, bass.ds(e, 1)]).then_inc(s["column_ready"], 1)

            v.wait_ge(s["route_ready"], 2)
            column(0, 0)
            column(0, 1)
            for n in range(2):
                yw_product(n, n)
                if n == 0:
                    column(1, 0)
                yw_low(n, n)
            for c in range(NCH):
                product(c, c % 2, c)
                if c:
                    low(c - 1, (c - 1) % 2, c - 1)

            def body(i, last):
                for u in range(4):
                    for c in range(NCH):
                        k = NCH * u + c
                        if not (last and u == 3):
                            product(i * (4 * NCH) + (k + 3), (k + 3) % 2, c)
                        if not (last and u == 3 and c > 0):
                            low(i * (4 * NCH) + (k + 2), k % 2, (c + 2) % NCH)
                        if c == 0 and not (last and u >= 2):
                            yw_product(i * 4 + (u + 2), u % 2)
                            if not (last and u >= 1):
                                column(i * 2 + (u + 3) // 2, (u + 3) % 2)
                        if c == 1 and not (last and u >= 2):
                            yw_low(i * 4 + (u + 2), u % 2)

            with v.Fori(0, E_ALL // 2 - 1) as i:
                body(i, False)
            body(E_ALL // 2 - 1, True)
            for half in range(HALVES):
                v.wait_ge(s["out_t"], half + 1)
                v.tensor_tensor(final[:, half * HT:(half + 1) * HT, :], tiles(ps[half][:]),
                                x2[:, half * HT:(half + 1) * HT, :], ALU.add
                                ).then_inc(s["out_ready"], 1)

        @block.tensor
        def _(pe):
            def per_half(f):
                for half in range(HALVES):
                    f(half)

            def spread(bank, column):
                for n in range(HT):
                    last = pe.transpose(bank[:, n * P:(n + 1) * P], lane(column(n), P), ident[:])
                return last

            pe.wait_ge(s["abs_ready"], 1)
            pe.wait_ge(s["const_ready"], 11)
            pe.matmul(ps[7][:, 0:4], ones[:], abs_sum[:], start=True, stop=True).then_inc(s["tot_ready"], 1)
            pe.wait_ge(s["in_xt"], 16)

            def cond_product(half):
                for k in range(3):
                    pe.wait_ge(gathered[k], OWNER[:(half + 1) * HB].count(k))
                for j in range(HB):
                    b = half * HB + j
                    last = pe.matmul(ps[4 * half][:, j * T:(j + 1) * T], cond_w[:, b, 0:D], x_ch[:, b, :],
                                     start=True, stop=True)
                last.then_inc(s["h_ps"], 1)
            per_half(cond_product)
            pe.wait_ge(s["ident_ready"], 1)
            pe.wait_ge(s["back_ready"], 1)

            def turn(half):
                for m in range(3):
                    pe.wait_ge(s["weighted_ready"], 3 * half + m + 1)
                    for n in range(HT):
                        last = pe.transpose(ps[4 * half + 1 + m][:, n * P:(n + 1) * P],
                                            weighted[:, half, m, n * P:(n + 1) * P], ident[:])
                    last.then_inc(s["weighted_t"], 1)
                for m in range(3):
                    pe.wait_ge(s["square_ready"], 3 * half + m + 1)
                    for n in range(HT):
                        last = pe.matmul(ps[4 * half][:, m * HT + n:m * HT + n + 1],
                                         square[:, half, m, n * P:(n + 1) * P], ones[:, 0:1],
                                         start=True, stop=True)
                last.then_inc(s["sumsq_ready"], 1)
            per_half(turn)

            def scale_out(half):
                pe.wait_ge(s["scale_ready"], 2 * half + 2)
                for m in range(3):
                    spread(ps[4 * half + 1 + m],
                           lambda n: stat[:, half, 6, m * HT + n:m * HT + n + 1]
                           ).then_inc(s["scale_bc"], 1)
            per_half(scale_out)

            def project(half):
                pe.wait_ge(s["w_q_ready"], 1)
                for m in range(3):
                    if m:
                        pe.wait_ge(s["back_sb"], 3 * half + m)
                    spread(ps[4 * half], lambda n: stat[:, half, 7, m * HT + n:m * HT + n + 1]
                           ).then_inc(s["back_bc"], 1)
                    pe.wait_ge(s["quant_ready"], 3 * half + m + 1)
                    pe.matmul(ps[4 * half + 1 + m][:], w_q[:, m, :], quant[:, half, m, :],
                              start=True, stop=True).then_inc(s["proj_ready"], 1)
            per_half(project)

            def turn_o(half):
                pe.wait_ge(s["wo_ready"], half + 1)
                for n in range(HT):
                    last = pe.transpose(ps[4 * half + 1][:, n * P:(n + 1) * P],
                                        weighted[:, half, 0, n * P:(n + 1) * P], ident[:])
                last.then_inc(s["wo_t"], 1)
                pe.wait_ge(s["sq_o"], half + 1)
                for n in range(HT):
                    last = pe.matmul(ps[4 * half][:, n:n + 1], square[:, half, 0, n * P:(n + 1) * P],
                                     ones[:, 0:1], start=True, stop=True)
                last.then_inc(s["sumsq_o"], 1)
            per_half(turn_o)

            def scale_out_o(half):
                pe.wait_ge(s["scale_o"], 2 * half + 2)
                spread(ps[4 * half + 2], lambda n: stat[:, half, 6, n:n + 1]).then_inc(s["bc_o"], 1)
            per_half(scale_out_o)

            def project_o(half):
                pe.wait_ge(s["quant_o"], half + 1)
                for n in range(HT):
                    last = pe.matmul(ps[4 * half + 3][:, n * D:(n + 1) * D],
                                     quant[:, half, 0, n * P:(n + 1) * P], w_q[:, 3, :],
                                     start=True, stop=True)
                last.then_inc(s["out_ps"], 1)
            per_half(project_o)

            def x2_turn(half):
                pe.wait_ge(s["x2_ready"], half + 1)
                for n in range(HT):
                    last = pe.transpose(ps[4 * half + 1][:, n * P:(n + 1) * P], x2[:, half * HT + n, :],
                                        ident[:])
                last.then_inc(s["x2_t_ps"], 1)
            per_half(x2_turn)
            pe.wait_ge(s["in_small"], 64)

            def score(half):
                pe.wait_ge(s["x2_t_ready"], half + 1)
                pe.matmul(ps[4 * half + 2][0:A_DIM, :], w1_sb[:], x2_t[:, half, :], start=True, stop=True
                          ).then_inc(s["w1_ps"], 1)
            per_half(score)

            def score_rows(half):
                pe.wait_ge(s["tanh_ready"], half + 1)
                pe.matmul(ps[4 * half][:], b1v[:, 1:2].broadcast_to([A_DIM, P]), tanh_t[:, half, :],
                          start=True, stop=True).then_inc(s["score_ps"], 1)
            per_half(score_rows)

            def pooled(half):
                pe.wait_ge(s["blocks_ready"], half + 1)
                for n in range(HT):
                    last = pe.matmul(ps[4 * half + 1][:, n * P:(n + 1) * P], x2[:, half * HT + n, :],
                                     blocks[:, half, n, :], start=True, stop=True)
                last.then_inc(s["pooled_ps"], 1)
            per_half(pooled)

            def logits(half):
                pe.wait_ge(s["y_ready"], half + 1)
                for n in range(HT):
                    last = pe.matmul(ps[4 * half + 2][:, n * E_ROUTED:(n + 1) * E_ROUTED],
                                     y[:, half, n * P:(n + 1) * P], wr[:], start=True, stop=True)
                last.then_inc(s["logit_ps"], 1)
            per_half(logits)

            def spread_route(n, half):
                pe.wait_ge(s["column_ready"], n + 1)
                spread(bc_ps[half], lambda t: route_col[:, half, t:t + 1]).then_inc(s["bc_ready"], 1)

            def three(bank, lhs, rhs, start, stop):
                for k, (a, b) in enumerate(((0, 0), (0, 1), (1, 0))):
                    last = pe.matmul(bank, lhs[a], rhs[b], start=start and k == 0, stop=stop and k == 2,
                                     skip_group_check=not start)
                return last

            def gate_up(buf, w, half, c):
                at, rows = CH[c]
                three(gate_ps[buf][0:rows, :], (w_hi[w][:, at:at + rows], w_lo[w][:, at:at + rows]),
                      (y_hi[:, half, :], y_lo[:, half, :]), True, True)
                at += HID
                three(up_ps[buf][0:rows, :], (w_hi[w][:, at:at + rows], w_lo[w][:, at:at + rows]),
                      (yw_hi[half][:], yw_lo[half][:]), True, True).then_inc(s["gu_ready"], 1)

            def down(w, half, c, stop):
                rows = CH[c][1]
                at = GU + c * D
                return three(acc_ps[half][:], (w_hi[w][0:rows, at:at + D], w_lo[w][0:rows, at:at + D]),
                             (hid_hi[c][0:rows, :], hid_lo[c][0:rows, :]), False, stop)

            spread_route(0, 0)
            spread_route(1, 1)
            for half in range(HALVES):
                pe.matmul(acc_ps[half][:], zeros[:, 0:P], zeros[:], start=True, stop=False,
                          skip_group_check=True)
            pe.wait_ge(s["y_split"], 2)
            pe.wait_ge(s["weight_split"], 1)
            pe.wait_ge(s["yw_split"], 1)
            for c in range(NCH):
                if c == 2:
                    pe.wait_ge(s["hid_ready"], 1)
                gate_up(c % 2, 0, 0, c)

            def body(i, last_body):
                for u in range(4):
                    w, half = u // 2, u % 2
                    final_unit = last_body and u == 3
                    nw, nhalf = ((u + 1) // 2) % 2, (u + 1) % 2
                    for c in range(NCH):
                        q = NCH * u + c
                        if not final_unit:
                            if c == 0:
                                pe.wait_ge(s["weight_split"], i * 2 + ((u + 1) // 2 + 1))
                                pe.wait_ge(s["yw_split"], i * 4 + (u + 2))
                            pe.wait_ge(s["hid_ready"], i * (4 * NCH) + (q + 2))
                            gate_up((q + 3) % 2, nw, nhalf, c)
                        if c == 0 and not (last_body and u >= 2):
                            pe.wait_ge(s["yw_ready"], i * 4 + (u + 1))
                            spread_route(i * 4 + (u + 2), u % 2)
                        pe.wait_ge(s["hid_split"], i * (4 * NCH) + (q + 1))
                        done = last_body and u >= 2 and c == NCH - 1
                        last = down(w, half, c, done)
                        if u % 2 == 1 and c == NCH - 1:
                            last.then_inc(s["expert_used"], 1)
                        elif done:
                            last.then_inc(s["acc_ready"], 1)

            with pe.Fori(0, E_ALL // 2 - 1) as i:
                body(i, False)
            body(E_ALL // 2 - 1, True)

            def out_turn(half):
                pe.wait_ge(s["acc_out"], half + 1)
                for n in range(HT):
                    last = pe.transpose(ps[half][:, n * P:(n + 1) * P], acc_sb[:, half, n * P:(n + 1) * P],
                                        ident[:])
                last.then_inc(s["out_t"], 1)
            per_half(out_turn)


def kernel(**inputs):
    import numpy as np
    import concourse.bacc as bacc
    from concourse.bass_utils import run_bass_kernel_spmd as run

    a = {k: np.asarray(v) for k, v in inputs.items()}
    attn = [a["L0_attn_" + n] for n in ("w_key", "w_value", "w_receptance", "w_output")]

    def experts_of(kind):
        return np.concatenate([a["L0_ffn_routed_" + kind], a["L0_ffn_shared_" + kind][None]])

    down = experts_of("down")
    padded = np.zeros((E_ALL, NCH * P, D), down.dtype)
    padded[:, :HID] = down
    arrays = {
        "x": a["x"],
        "x_t": a["x"].reshape(B * T, D).T,
        "subject": a["itok_B_0_15"].reshape(1, B),
        "prompt_type": a["itok_B_0_2"].reshape(TILES, 4).T,
        "cond": np.concatenate([a["L0_cond_weights"], a["L0_cond_b"][:, :, None]], axis=2
                               ).transpose(1, 0, 2).reshape(D, SUBJECTS * (D + 1)),
        "cols": np.stack([a["L0_attn_" + n].reshape(D) for n in (
            "time_decay", "time_first", "time_mix_key", "time_mix_value", "time_mix_receptance",
            "rms_key", "rms_value", "rms_receptance", "rms_output")], axis=1),
        "attn_w": np.concatenate([w.T for w in attn], axis=1),
        "w1": a["L0_cond2_W1"],
        "b1_v": np.stack([a["L0_cond2_b1"], a["L0_cond2_v"]], axis=1),
        "router_w": a["L0_ffn_Wr"],
        "router_b": a["L0_ffn_routing_bias"].reshape(1, E_ROUTED),
        "experts": np.concatenate(
            [experts_of("gate"), experts_of("up"),
             padded.reshape(E_ALL, NCH, P, D).transpose(0, 2, 1, 3).reshape(E_ALL, P, NCH * D)], axis=2),
    }
    nc = bacc.Bacc("TRN2", target_bir_lowering=False, num_devices=1)
    feed, args = {}, []
    for name, value in arrays.items():
        value = np.ascontiguousarray(value)
        feed["in_" + name] = value
        args.append(nc.dram_tensor("in_" + name, value.shape, mybir.dt.from_np(value.dtype),
                                   kind="ExternalInput").ap())
    out = nc.dram_tensor("out_0", (B, T, D), F32, kind="ExternalOutput").ap()
    adaln_attention_ffn(nc, *args, out)
    return run(nc, [feed], core_ids=[0]).results[0]["out_0"]
```

```python
from contextlib import ExitStack

import concourse.bass as bass
from concourse import mybir

ALU = mybir.AluOpType
ACT = mybir.ActivationFunctionType
AX_X = mybir.AxisListType.X
F32 = mybir.dt.float32
F32R = mybir.dt.float32r
BF16 = mybir.dt.bfloat16
I32 = mybir.dt.int32

P = 128
B, T, D = 32, 32, 128
SUBJECTS = 16
GATHER = {"vector": (0, 7), "scalar": (7, 14), "gpsimd": (14, 16)}
TILES = B * T // P
HALVES = 2
HB = B // HALVES
HT = TILES // HALVES
N = HB * T
TP = T + 1
HID = 352
CH = [(0, 128), (128, 128), (256, HID - 256)]
NCH = len(CH)
E_ROUTED = 7
E_ALL = E_ROUTED + 1
A_DIM = 32
GU = 2 * HID
PACK = GU + NCH * D
ROUND = 12582912.0
RMS_EPS = 1e-8
TINY = 1e-5
WIDE = 128
BIG = 1e30
COL = {n: i for i, n in enumerate(
    ["decay", "first", "mix_k", "mix_v", "mix_r", "rms_k", "rms_v", "rms_r", "rms_o"])}


def adaln_attention_ffn(nc, x, x_t, subject, prompt_type, cond, cols, attn_w, w1, b1_v,
                        router_w, router_b, experts, out):
    ctx = ExitStack()
    with ctx:
        def sb(name, shape, dt=F32):
            return ctx.enter_context(nc.sbuf_tensor(name, shape, dt))

        def sem(name):
            return ctx.enter_context(nc.semaphore(name))

        x_tok = sb("x_tok", [P, TILES, D])
        x_ch = sb("x_ch", [P, B, T])
        subj = sb("subj", [1, B], I32)
        ptype_i = sb("ptype_i", [P, TILES], I32)
        cond_w = sb("cond_w", [P, B, D + 1])
        vec = sb("vec", [P, len(COL)])
        aw = sb("aw", [P, 4, D])
        w1_sb = sb("w1_sb", [P, A_DIM])
        b1v = sb("b1v", [A_DIM, 2])
        wr = sb("wr", [P, WIDE])
        rbias = sb("rbias", [P, E_ROUTED])
        raw = sb("raw", [P, 2, PACK])
        cond_all = raw[:].rearrange("p b n -> p (b n)")[:, 0:SUBJECTS * (D + 1)].rearrange(
            "p (s d) -> p s d", s=SUBJECTS)

        ident = sb("ident", [P, P])
        ones = sb("ones", [P, P])
        zeros = sb("zeros", [P, N], BF16)
        zero_col = sb("zero_col", [P, 1])
        neg_half = sb("neg_half", [P, 3 * HT])
        diff = sb("diff", [P, T])
        below = sb("below", [P, T])
        above = sb("above", [P, T])
        other = sb("other", [P, T])
        ptype = sb("ptype", [P, TILES])
        is_kind = sb("is_kind", [P, 3, TILES])
        mask = sb("mask", [P, TILES, T])
        mask_b = sb("mask_b", [P, TILES, T])
        penalty = sb("penalty", [P, TILES, T])
        count = sb("count", [P, TILES])
        rank = sb("rank", [P, E_ROUTED])
        one_less = sb("one_less", [P, 3])
        decay = sb("decay", [P, 1])
        log_w = sb("log_w", [P, 1])
        scan_w = sb("scan_w", [P, HB, TP])

        abs_sum = sb("abs_sum", [P, 4])
        w_mean = sb("w_mean", [P, 4])
        w_scale = sb("w_scale", [P, 4])
        w_back = sb("w_back", [P, 4])
        w_round = sb("w_round", [P, 4, D])
        w_clip = sb("w_clip", [P, 4, D])
        w_q = sb("w_q", [P, 4, D], BF16)

        h_pad = sb("h_pad", [P, HALVES, HB, TP])
        shifted = sb("shifted", [P, HALVES, 3, N])
        mixed = sb("mixed", [P, HALVES, 3, N])
        square = sb("square", [P, HALVES, 3, N])
        weighted = sb("weighted", [P, HALVES, 3, N])
        scaled = mixed
        quant = sb("quant", [P, HALVES, 3, N], BF16)
        stat = sb("stat", [P, HALVES, 8, 3 * HT])
        back = square
        k_pad = sb("k_pad", [P, HALVES, HB, TP])
        val, rec, exp_r = (shifted[:, :, m, :] for m in range(3))
        eps = sb("eps", [P, HALVES, HB, TP])
        dec_arg, new_arg = weighted[:, :, 1, :], weighted[:, :, 2, :]
        dec_pad = sb("dec_pad", [P, HALVES, HB, TP])
        new_pad = sb("new_pad", [P, HALVES, HB, TP])
        newv_pad = sb("newv_pad", [P, HALVES, HB, TP])
        alpha = sb("alpha", [P, HALVES, HB, TP])
        beta = sb("beta", [P, HALVES, HB, TP])
        tau, arg = mixed[:, :, 0, :], mixed[:, :, 1:3, :]
        e12 = sb("e12", [P, HALVES, 2, N])
        prod = cond_w[:].rearrange("p b d -> p (b d)")[:, 0:HALVES * 4 * N].rearrange(
            "p (h k n) -> p h k n", h=HALVES, k=4)
        mixed_o = weighted[:, :, 2, :]
        x2 = sb("x2", [P, TILES, D])
        x2_t = weighted[:, :, 1, :]
        tanh_t = sb("tanh_t", [A_DIM, HALVES, N])
        scores = sb("scores", [P, HALVES, HT, T])
        soft = sb("soft", [P, HALVES, HT, T])
        soft_n = sb("soft_n", [P, HALVES, HT, T])
        row = sb("row", [P, HALVES, 4, HT])
        blocks = sb("blocks", [P, HALVES, HT, P])
        y = x_ch[:].rearrange("p (h b) t -> p h (b t)", h=HALVES)
        y_hi = sb("y_hi", [P, HALVES, N], F32R)
        y_lo = sb("y_lo", [P, HALVES, N], F32R)
        gate_e = sb("gate_e", [P, 8, TILES, E_ROUTED])
        gate_t = sb("gate_t", [P, 8, TILES])
        route = sb("route", [P, TILES, E_ROUTED])
        route_col = sb("route_col", [P, HALVES, HT])

        w_hi = [sb(f"w_hi{i}", [P, PACK], F32R) for i in range(2)]
        w_lo = [sb(f"w_lo{i}", [P, PACK], F32R) for i in range(2)]
        yw = mixed[:, 0, 2, :]
        yw_hi = [sb(f"yw_hi{i}", [P, N], F32R) for i in range(2)]
        yw_lo = [sb(f"yw_lo{i}", [P, N], F32R) for i in range(2)]
        silu, hid = mixed[:, 0, 0:2, :], mixed[:, 1, 0:2, :]
        hid_hi = [sb(f"hid_hi{i}", [P, N], F32R) for i in range(NCH)]
        hid_lo = [sb(f"hid_lo{i}", [P, N], F32R) for i in range(NCH)]
        acc_sb = square[:, :, 0, :]
        final = weighted[:].rearrange("p h m n -> p (h m n)")[:, 0:TILES * D].rearrange(
            "p (n d) -> p n d", n=TILES)

        ps = [ctx.enter_context(nc.psum_tensor(f"ps{i}", [P, 512], F32)) for i in range(8)]
        gate_ps, up_ps, bc_ps, acc_ps = ps[0:2], ps[2:4], ps[4:6], ps[6:8]

        def tiles(ap):
            return ap.rearrange("p (n c) -> p n c", n=HT)

        def steps(ap):
            return ap.rearrange("p (b t) -> p b t", t=T)

        def lane(ap, n):
            return ap.broadcast_to([P, n])

        names = """in_subj in_vec in_aw in_small in_x in_type in_cond stored
            const_ready zeros_ready zero_ready ident_ready one_less_done decay_done log_w_ready scan_ready abs_ready
            tot_ready w_mean_ready w_q_ready back_ready penalty_ready count_ready ptype_ready
            h_ps h_ready shift_ready mix_ready square_ready weighted_ready weighted_r weighted_t sumsq_ready
            meansq_ready rms_ready scale_ready scale_bc quant_ready proj_ready back_bc back_sb
            k_ready eps_ready val_ready newv_ready e2v_ready r_ready exp_r_ready dec_arg_ready new_arg_ready dec_ready new_ready
            old_arg_ready new_u_arg_ready e1_ready e2_ready tau_ready alpha_ready old_v_ready numerator_ready o_ready sq_o wo_ready wo_t sumsq_o meansq_o rms_o scale_o
            bc_o quant_o out_ps x2_ready x2_t_ps x2_t_ready w1_ps tanh_ready score_ps
            soft_arg exp_s blocks_ready pooled_ps y_ready y_hi_ready y_split logit_ps
            exp_l route_ready vec_step pool_step pool_in
            weight_split column_ready expert_used bc_ready yw_ready yw_hi_ready yw_split gu_ready silu_ready
            hid_ready hid_hi_ready hid_split acc_ready acc_out out_t out_ready""".split()
        s = {n: sem(n) for n in names}

        gathered = {k: sem("gathered_" + k) for k in GATHER}
        table = "a subject's number is a row of the table of subjects"

        def gather(name, engine, eng, copy):
            first, end = GATHER[name]
            eng.wait_ge(s["in_subj"], 16)
            who = [nc.values_load_multi_w_load_instructions(
                subj[0:1, half * HB + first:half * HB + end], engines=[engine], min_val=0,
                max_val=SUBJECTS - 1, skip_runtime_bounds_check_because=table)[1]
                for half in range(HALVES)]
            eng.wait_ge(s["in_cond"], 16)
            for half in range(HALVES):
                for k in range(end - first):
                    b = half * HB + first + k
                    copy(cond_w[:, b:b + 1, :], cond_all[:, bass.ds(who[half][k], 1), :]
                         ).then_inc(gathered[name], 1)

        in_xt = [sem(f"in_xt{h}") for h in range(HALVES)]
        expert_in = [sem(f"expert_in{b}") for b in range(2)]

        block = ctx.enter_context(nc.Block())

        @block.sync
        def _(sp):
            sp.dma_start(subj[:], subject).then_inc(s["in_subj"], 16)
            sp.dma_start(cond_all[:].rearrange("p s d -> p (s d)"), cond).then_inc(s["in_cond"], 16)
            x_half = x_ch[:].rearrange("p (h b) t -> p h (b t)", h=HALVES)
            sp.dma_start(x_half[:, 0, :], x_t[:, 0:N]).then_inc(in_xt[0], 16)
            sp.dma_start(aw[:].rearrange("p m d -> p (m d)"), attn_w).then_inc(s["in_aw"], 16)
            sp.dma_start(x_half[:, 1, :], x_t[:, N:]).then_inc(in_xt[1], 16)
            for g in range(4):
                sp.dma_start(ptype_i[32 * g:32 * g + 32, :],
                             prompt_type[g:g + 1, :].broadcast_to([32, TILES])
                             ).then_inc(s["in_type"], 16)
            sp.dma_start(x_tok[:], x.rearrange("b t d -> (b t) d").rearrange("(n p) d -> p n d", p=P)
                         ).then_inc(s["in_x"], 16)
            sp.dma_start(w1_sb[:], w1).then_inc(s["in_small"], 16)
            sp.dma_start(b1v[:], b1_v).then_inc(s["in_small"], 16)
            sp.dma_start(wr[:, 0:E_ROUTED], router_w).then_inc(s["in_small"], 16)
            sp.dma_start(rbias[:], router_b.broadcast_to([P, E_ROUTED])).then_inc(s["in_small"], 16)
            for k, (first, end) in GATHER.items():
                sp.wait_ge(gathered[k], HALVES * (end - first))
            for e in range(2):
                sp.dma_start(raw[:, e, :], experts[e]).then_inc(expert_in[e], 16)
            with sp.Fori(0, E_ALL // 2 - 1) as i:
                for b in range(2):
                    sp.wait_ge(s["weight_split"], i * 2 + (b + 1))
                    sp.dma_start(raw[:, b, :], experts[bass.ds(i * 2 + (b + 2), 1)].rearrange(
                        "e p n -> p (e n)")).then_inc(expert_in[b], 16)
            sp.wait_ge(s["out_ready"], 1)
            o_v = out.rearrange("b t d -> (b t) d").rearrange("(n p) d -> p n d", p=P)
            sp.dma_start(o_v[:, 0:HT, :], final[:, 0:HT, :]).then_inc(s["stored"], 16)
            sp.wait_ge(s["out_ready"], 2)
            sp.dma_start(o_v[:, HT:, :], final[:, HT:, :]).then_inc(s["stored"], 16)
            sp.wait_ge(s["stored"], 32)

        @block.gpsimd
        def _(pool):
            step = [0]

            def then(ins):
                step[0] += 1
                ins.then_inc(s["pool_step"], 1)
                pool.wait_ge(s["pool_step"], step[0])

            pool.memset(zeros[:], 0.0).then_inc(s["zeros_ready"], 1)
            pool.memset(ident[:], 0.0).then_inc(s["zero_ready"], 1)
            pool.wait_ge(s["zero_ready"], 1)
            pool.affine_select(out=ident[:], in_=ident[:], compare_op=ALU.not_equal, fill=1.0, base=0,
                               pattern=[[-1, P]], channel_multiplier=1).then_inc(s["ident_ready"], 1)
            pool.memset(ones[:], 1.0).then_inc(s["const_ready"], 1)
            pool.memset(zero_col[:], 0.0).then_inc(s["const_ready"], 1)
            pool.memset(wr[:, E_ROUTED:], 0.0).then_inc(s["const_ready"], 1)
            pool.memset(neg_half[:], -0.5).then_inc(s["const_ready"], 1)
            pool.memset(h_pad[:, :, :, 0:1], 0.0).then_inc(s["const_ready"], 1)
            pool.memset(k_pad[:, :, :, 0:1], 0.0).then_inc(s["const_ready"], 1)
            pool.memset(dec_pad[:, :, :, 0:1], 0.0).then_inc(s["const_ready"], 1)
            pool.memset(new_pad[:, :, :, 0:1], 0.0).then_inc(s["const_ready"], 1)
            pool.memset(newv_pad[:, :, :, 0:1], 0.0).then_inc(s["const_ready"], 1)
            pool.memset(blocks[:], 0.0).then_inc(s["const_ready"], 1)
            pool.wait_ge(s["const_ready"], 10)
            for g in range(4):
                then(pool.iota(diff[32 * g:32 * g + 32, :], pattern=[[1, T]], base=0,
                               channel_multiplier=-1, allow_small_or_imprecise_dtypes=True))
            then(pool.iota(rank[:], pattern=[[-1, E_ROUTED]], base=E_ROUTED, channel_multiplier=0,
                           allow_small_or_imprecise_dtypes=True))
            then(pool.tensor_scalar(below[:], diff[:], 0.0, None, ALU.is_le))
            then(pool.tensor_scalar(above[:], diff[:], 0.0, None, ALU.is_ge))
            then(pool.tensor_tensor(other[:], below[:], above[:], ALU.add))
            then(pool.tensor_scalar(other[:], other[:], -1.0, 2.0, ALU.mult, ALU.add))
            gather("gpsimd", mybir.EngineType.Pool, pool, pool.tensor_copy)
            pool.wait_ge(s["in_type"], 64)
            then(pool.tensor_copy(ptype[:], ptype_i[:]))
            then(pool.tensor_scalar(is_kind[:, 0, :], ptype[:], 0.0, None, ALU.is_equal))
            then(pool.tensor_scalar(is_kind[:, 1, :], ptype[:], 1.0, None, ALU.is_equal))
            then(pool.tensor_tensor(is_kind[:, 2, :], is_kind[:, 0, :], is_kind[:, 1, :], ALU.add))
            then(pool.tensor_scalar(is_kind[:, 2, :], is_kind[:, 2, :], -1.0, 1.0, ALU.mult, ALU.add))
            shape = [P, TILES, T]

            def term(dst, kind, rows):
                then(pool.tensor_tensor(dst[:], is_kind[:, kind, :].unsqueeze(2).broadcast_to(shape),
                                        rows[:].unsqueeze(1).broadcast_to(shape), ALU.mult))
            term(mask, 0, below)
            term(mask_b, 1, above)
            then(pool.tensor_tensor(mask[:], mask[:], mask_b[:], ALU.add))
            term(mask_b, 2, other)
            then(pool.tensor_tensor(mask[:], mask[:], mask_b[:], ALU.add))
            pool.tensor_scalar(penalty[:], mask[:], BIG, -BIG, ALU.mult, ALU.add
                               ).then_inc(s["penalty_ready"], 1)
            for half in range(HALVES):
                pool.wait_ge(s["mix_ready"], 3 * half + 3)
                pool.tensor_tensor(weighted[:, half, 2, :], mixed[:, half, 2, :],
                                   vec[:, 7:8].broadcast_to([P, N]), ALU.mult
                                   ).then_inc(s["weighted_r"], 1)
            for half in range(HALVES):
                pool.wait_ge(s["meansq_ready"], half + 1)
                pool.tensor_tensor(stat[:, half, 1, :], stat[:, half, 0, :], neg_half[:], ALU.pow
                                   ).then_inc(s["rms_ready"], 1)
            def minus(dst, a, b, done):
                pool.tensor_tensor(dst, a, b, ALU.subtract).then_inc(s[done], 1)

            def wkv_args(half):
                old, new = eps[:, half, :, 0:T], eps[:, half, :, 1:TP]
                pool.wait_ge(s["eps_ready"], half + 1)
                minus(steps(dec_arg[:, half, :]), old, new, "dec_arg_ready")
                minus(steps(new_arg[:, half, :]), k_pad[:, half, :, 1:TP], new, "new_arg_ready")
                pool.wait_ge(s["tau_ready"], half + 1)
                minus(steps(arg[:, half, 0, :]), old, steps(tau[:, half, :]), "old_arg_ready")

            def values(half):
                pool.wait_ge(s["new_ready"], half + 1)
                pool.wait_ge(s["val_ready"], half + 1)
                pool.tensor_tensor(newv_pad[:, half, :, 1:TP], new_pad[:, half, :, 1:TP],
                                   steps(val[:, half, :]), ALU.mult).then_inc(s["newv_ready"], 1)
                pool.wait_ge(s["e2_ready"], half + 1)
                pool.tensor_tensor(prod[:, half, 2, :], e12[:, half, 1, :], val[:, half, :], ALU.mult
                                   ).then_inc(s["e2v_ready"], 1)

            def numerator(half):
                pool.wait_ge(s["e1_ready"], half + 1)
                pool.wait_ge(s["alpha_ready"], half + 1)
                pool.tensor_tensor(steps(prod[:, half, 1, :]), steps(e12[:, half, 0, :]),
                                   alpha[:, half, :, 0:T], ALU.mult).then_inc(s["old_v_ready"], 1)
                pool.wait_ge(s["old_v_ready"], half + 1)
                pool.wait_ge(s["e2v_ready"], half + 1)
                pool.tensor_tensor(prod[:, half, 1, :], prod[:, half, 1, :], prod[:, half, 2, :],
                                   ALU.add).then_inc(s["numerator_ready"], 1)

            wkv_args(0)
            values(0)
            wkv_args(1)
            numerator(0)
            values(1)
            numerator(1)
            for half in range(HALVES):
                pool.wait_ge(s["meansq_o"], half + 1)
                pool.tensor_tensor(stat[:, half, 1, 0:HT], stat[:, half, 0, 0:HT], neg_half[:, 0:HT],
                                   ALU.pow).then_inc(s["rms_o"], 1)

            def split(e, pair, b):
                w = raw[:, b, :]
                pool.wait_ge(expert_in[b], (pair + 1) * 16)
                pool.tensor_tensor(w_hi[b][:], w, zero_col[:].broadcast_to([P, PACK]), ALU.add).then_inc(s["pool_in"], 1)
                pool.wait_ge(s["pool_in"], e + 1)
                pool.tensor_tensor(w_lo[b][:], w, w_hi[b][:].bitcast(F32), ALU.subtract
                                   ).then_inc(s["weight_split"], 1)
            split(0, 0, 0)
            split(1, 0, 1)
            with pool.Fori(0, E_ALL // 2 - 1) as i:
                for b in range(2):
                    pool.wait_ge(s["expert_used"], i * 2 + (b + 1))
                    split(i * 2 + (b + 2), i + 1, b)

        @block.scalar
        def _(act):
            act.dma_start(vec[:], cols).then_inc(s["in_vec"], 16)
            act.wait_ge(s["in_vec"], 16)
            act.activation(decay[:], vec[:, 0:1], ACT.Exp).then_inc(s["decay_done"], 1)
            gather("scalar", mybir.EngineType.Activation, act,
                   lambda o, x: act.activation(o, x, ACT.Copy))

            def per_half(f):
                for half in range(HALVES):
                    f(half)

            def shift(half):
                act.wait_ge(s["h_ready"], half + 1)
                act.wait_ge(s["one_less_done"], 1)
                for m in range(3):
                    act.activation(steps(shifted[:, half, m, :]), h_pad[:, half, :, 0:T], ACT.Identity,
                                   scale=one_less[:, m:m + 1]).then_inc(s["shift_ready"], 1)

            def squares(half):
                for m in range(3):
                    act.wait_ge(s["mix_ready"], 3 * half + m + 1)
                    act.activation(square[:, half, m, :], mixed[:, half, m, :], ACT.Square
                                   ).then_inc(s["square_ready"], 1)
            for half in range(HALVES):
                shift(half)
                squares(half)

            def backs(half):
                for m in range(3):
                    act.wait_ge(s["back_bc"], 3 * half + m + 1)
                    act.activation(back[:, half, m, :], ps[4 * half][:], ACT.Copy
                                   ).then_inc(s["back_sb"], 1)
            per_half(backs)

            def exps(half):
                act.wait_ge(s["dec_arg_ready"], half + 1)
                act.activation(dec_pad[:, half, :, 1:TP], steps(dec_arg[:, half, :]), ACT.Exp,
                               bias=log_w[:, 0:1]).then_inc(s["dec_ready"], 1)
                act.wait_ge(s["new_arg_ready"], half + 1)
                act.activation(new_pad[:, half, :, 1:TP], steps(new_arg[:, half, :]), ACT.Exp
                               ).then_inc(s["new_ready"], 1)
                act.wait_ge(s["new_u_arg_ready"], half + 1)
                act.activation(e12[:, half, 1, :], arg[:, half, 1, :], ACT.Exp
                               ).then_inc(s["e2_ready"], 1)
                act.wait_ge(s["old_arg_ready"], half + 1)
                act.activation(e12[:, half, 0, :], arg[:, half, 0, :], ACT.Exp
                               ).then_inc(s["e1_ready"], 1)
                act.wait_ge(s["r_ready"], half + 1)
                act.activation(exp_r[:, half, :], rec[:, half, :], ACT.Exp, scale=-1.0
                               ).then_inc(s["exp_r_ready"], 1)
            per_half(exps)

            def weigh_o(half):
                act.wait_ge(s["o_ready"], half + 1)
                act.activation(square[:, half, 0, :], mixed_o[:, half, :], ACT.Square
                               ).then_inc(s["sq_o"], 1)
                act.activation(weighted[:, half, 0, :], mixed_o[:, half, :], ACT.Identity,
                               scale=vec[:, 8:9]).then_inc(s["wo_ready"], 1)
            per_half(weigh_o)

            def x2_copy(half):
                act.wait_ge(s["x2_t_ps"], half + 1)
                act.activation(x2_t[:, half, :], ps[4 * half + 1][:], ACT.Copy
                               ).then_inc(s["x2_t_ready"], 1)

            def score_tanh(half):
                act.wait_ge(s["w1_ps"], half + 1)
                act.wait_ge(s["in_small"], 64)
                act.activation(tanh_t[:, half, :], ps[4 * half + 2][0:A_DIM, :], ACT.Tanh,
                               bias=b1v[:, 0:1]).then_inc(s["tanh_ready"], 1)

            def softmax(half):
                act.wait_ge(s["soft_arg"], half + 1)
                act.activation(soft[:, half], scores[:, half], ACT.Exp).then_inc(s["exp_s"], 1)

            x2_copy(0)
            score_tanh(0)
            x2_copy(1)
            softmax(0)
            score_tanh(1)
            softmax(1)

            def y_copy(half):
                act.wait_ge(s["pooled_ps"], half + 1)
                act.activation(y[:, half, :], ps[4 * half + 1][:], ACT.Copy).then_inc(s["y_ready"], 1)
                act.activation(y_hi[:, half, :], ps[4 * half + 1][:], ACT.Copy
                               ).then_inc(s["y_hi_ready"], 1)
            per_half(y_copy)
            act.activation(yw_hi[1][:], ps[5][:], ACT.Copy).then_inc(s["y_hi_ready"], 1)
            act.wait_ge(s["yw_ready"], 2)
            act.activation(gate_e[:, 1], gate_e[:, 0], ACT.Exp, scale=-1.0).then_inc(s["exp_l"], 1)

            def yw_high(n, b):
                act.wait_ge(s["yw_ready"], n + 1)
                act.activation(yw_hi[b][:], yw, ACT.Copy).then_inc(s["yw_hi_ready"], 1)

            def chunk(q, b, c):
                rows = CH[c][1]
                act.wait_ge(s["gu_ready"], q + 1)
                act.activation(silu[0:rows, b, :], gate_ps[b][0:rows, :], ACT.Silu
                               ).then_inc(s["silu_ready"], 1)

            def high(q, b, c):
                rows = CH[c][1]
                act.wait_ge(s["hid_ready"], q + 1)
                act.activation(hid_hi[c][0:rows, :], hid[0:rows, b, :], ACT.Copy
                               ).then_inc(s["hid_hi_ready"], 1)

            for c in range(NCH):
                chunk(c, c % 2, c)
                if c:
                    high(c - 1, (c - 1) % 2, c - 1)

            def body(i, last):
                for u in range(4):
                    for c in range(NCH):
                        k = NCH * u + c
                        if not (last and u == 3):
                            chunk(i * (4 * NCH) + (k + 3), (k + 3) % 2, c)
                        if last and u == 3 and c == 0:
                            act.wait_ge(s["acc_ready"], 1)
                        if not (last and u == 3 and c > 0):
                            high(i * (4 * NCH) + (k + 2), k % 2, (c + 2) % NCH)
                        if c == 0 and not (last and u >= 2):
                            yw_high(i * 4 + (u + 2), u % 2)

            with act.Fori(0, E_ALL // 2 - 1) as i:
                body(i, False)
            body(E_ALL // 2 - 1, True)
            for half in range(HALVES):
                act.wait_ge(*((s["acc_ready"], 1) if half == 0 else (s["expert_used"], E_ALL)))
                act.activation(acc_sb[:, half, :], acc_ps[half][:], ACT.Copy).then_inc(s["acc_out"], 1)

        @block.vector
        def _(v):
            step = [0]

            def then(ins):
                step[0] += 1
                ins.then_inc(s["vec_step"], 1)
                v.wait_ge(s["vec_step"], step[0])

            def weight_sums():
                v.wait_ge(s["in_aw"], 16)
                v.tensor_reduce(abs_sum[:], aw[:], AX_X, ALU.add, apply_absolute_value=True
                                ).then_inc(s["abs_ready"], 1)

            def note(ins):
                step[0] += 1
                ins.then_inc(s["vec_step"], 1)
                return step[0]

            gather("vector", mybir.EngineType.DVE, v, v.tensor_copy)
            weight_sums()
            v.wait_ge(s["in_vec"], 16)
            v.tensor_scalar(one_less[:], vec[:, 2:5], -1.0, 1.0, ALU.mult, ALU.add
                            ).then_inc(s["one_less_done"], 1)
            v.wait_ge(s["decay_done"], 1)
            v.tensor_scalar(log_w[:], decay[:], -1.0, None, ALU.mult).then_inc(s["log_w_ready"], 1)
            v.wait_ge(s["log_w_ready"], 1)
            v.wait_ge(s["const_ready"], 10)
            then(v.tensor_scalar(scan_w[:, :, 1:TP], h_pad[:, 0, :, 0:1].broadcast_to([P, HB, T]),
                                 log_w[:, 0:1], None, ALU.add))
            v.memset(scan_w[:, :, 0:1], -BIG).then_inc(s["scan_ready"], 1)
            def per_half(f):
                for half in range(HALVES):
                    f(half)

            def h_out(half):
                v.wait_ge(s["h_ps"], half + 1)
                v.tensor_tensor(h_pad[:, half, :, 1:TP], steps(ps[4 * half][:]),
                                cond_w[:, half * HB:(half + 1) * HB, D:D + 1].broadcast_to([P, HB, T]),
                                ALU.add).then_inc(s["h_ready"], 1)

            def mix(half):
                v.wait_ge(s["h_ready"], half + 1)
                for m in range(3):
                    v.wait_ge(s["shift_ready"], 3 * half + m + 1)
                    v.scalar_tensor_tensor(out=steps(mixed[:, half, m, :]), in0=h_pad[:, half, :, 1:TP],
                                           scalar=vec[:, 2 + m:3 + m], in1=steps(shifted[:, half, m, :]),
                                           op0=ALU.mult, op1=ALU.add).then_inc(s["mix_ready"], 1)

            def weigh(half):
                for m in range(2):
                    v.wait_ge(s["mix_ready"], 3 * half + m + 1)
                    v.tensor_scalar(weighted[:, half, m, :], mixed[:, half, m, :], vec[:, 5 + m:6 + m],
                                    None, ALU.mult).then_inc(s["weighted_ready"], 1)
            h_out(0)
            mix(0)
            v.wait_ge(s["tot_ready"], 1)
            v.tensor_scalar(w_mean[:], ps[7][:, 0:4], 1.0 / (D * D), TINY, ALU.mult, ALU.max
                            ).then_inc(s["w_mean_ready"], 1)
            h_out(1)
            weigh(0)
            mix(1)
            weigh(1)

            def mean_squares(half, n, sumsq, meansq_sem):
                v.wait_ge(sumsq[0], half + 1)
                v.tensor_scalar(stat[:, half, 0, 0:n], sumsq[1], 1.0 / D, RMS_EPS, ALU.mult, ALU.add
                                ).then_inc(meansq_sem, 1)

            def peaks(half, n, turned):
                for m in range(n // HT):
                    v.wait_ge(turned, n // HT * half + m + 1)
                    last = v.tensor_reduce(stat[:, half, 2, HT * m:HT * m + HT],
                                           tiles(ps[4 * half + 1 + m][:]), AX_X, ALU.max,
                                           apply_absolute_value=True)
                then(last)

            def scale_rows(half, n, rms_sem, back_w, done):
                st = stat[:, half]
                v.wait_ge(rms_sem, half + 1)
                then(v.tensor_tensor(st[:, 3, 0:n], st[:, 2, 0:n], st[:, 1, 0:n], ALU.mult))
                then(v.tensor_scalar(st[:, 4, 0:n], st[:, 3, 0:n], TINY, None, ALU.max))
                then(v.reciprocal(st[:, 5, 0:n], st[:, 4, 0:n]))
                v.scalar_tensor_tensor(out=st[:, 6, 0:n], in0=st[:, 1, 0:n], scalar=127.0,
                                       in1=st[:, 5, 0:n], op0=ALU.mult, op1=ALU.mult).then_inc(done, 1)
                v.tensor_tensor(st[:, 7, 0:n].rearrange("p (m n) -> p m n", n=HT),
                                st[:, 4, 0:n].rearrange("p (m n) -> p m n", n=HT), back_w,
                                ALU.mult).then_inc(done, 1)

            def quantise_weights():
                v.wait_ge(s["w_mean_ready"], 1)
                then(v.reciprocal(w_scale[:], w_mean[:]))
                v.tensor_scalar(w_back[:], w_mean[:], 1.0 / 127.0, None, ALU.mult).then_inc(s["back_ready"], 1)
                for m in range(4):
                    last = v.tensor_scalar(w_round[:, m, :], aw[:, m, :], w_scale[:, m:m + 1], ROUND,
                                           ALU.mult, ALU.add)
                then(last)
                then(v.tensor_scalar(w_clip[:], w_round[:], -ROUND, 1.0, ALU.add, ALU.min))
                v.tensor_scalar(w_q[:], w_clip[:], -1.0, None, ALU.max).then_inc(s["w_q_ready"], 1)

            for half in range(HALVES):
                mean_squares(half, 3 * HT, (s["sumsq_ready"], ps[4 * half][:, 0:3 * HT]),
                             s["meansq_ready"])
                peaks(half, 3 * HT, s["weighted_t"])
                if half == 0:
                    quantise_weights()
            v.wait_ge(s["back_ready"], 1)
            for half in range(HALVES):
                scale_rows(half, 3 * HT, s["rms_ready"],
                           w_back[:, 0:3].unsqueeze(2).broadcast_to([P, 3, HT]), s["scale_ready"])

            def quantise(half):
                got = [0] * 3
                for m in range(4):
                    if m < 3:
                        v.wait_ge(s["scale_bc"], 3 * half + m + 1)
                        v.wait_ge(*((s["weighted_ready"], 2 * half + m + 1) if m < 2 else
                                    (s["weighted_r"], half + 1)))
                        got[m] = note(v.tensor_tensor(scaled[:, half, m, :], weighted[:, half, m, :],
                                                      ps[4 * half + 1 + m][:], ALU.mult))
                    if m:
                        v.wait_ge(s["vec_step"], got[m - 1])
                        v.tensor_scalar(quant[:, half, m - 1, :], scaled[:, half, m - 1, :], ROUND, -ROUND,
                                        ALU.add, ALU.add).then_inc(s["quant_ready"], 1)
            per_half(quantise)

            def wkv_args(half):
                v.wait_ge(s["proj_ready"], 3 * half + 1)
                v.wait_ge(s["back_sb"], 3 * half + 1)
                v.tensor_tensor(k_pad[:, half, :, 1:TP], steps(ps[4 * half + 1][:]),
                                steps(back[:, half, 0, :]), ALU.mult).then_inc(s["k_ready"], 1)
                v.wait_ge(s["k_ready"], half + 1)
                v.wait_ge(s["scan_ready"], 1)
                flat = "p b t -> p (b t)"
                v.tensor_tensor_scan(eps[:, half].rearrange(flat), scan_w[:].rearrange(flat),
                                     k_pad[:, half].rearrange(flat), 0.0, ALU.add, ALU.max
                                     ).then_inc(s["eps_ready"], 1)
                v.wait_ge(s["eps_ready"], half + 1)
                old, k = eps[:, half, :, 0:T], k_pad[:, half, :, 1:TP]
                v.scalar_tensor_tensor(out=steps(tau[:, half, :]), in0=k, scalar=vec[:, 1:2], in1=old,
                                       op0=ALU.add, op1=ALU.max).then_inc(s["tau_ready"], 1)
                v.wait_ge(s["tau_ready"], half + 1)
                v.scalar_tensor_tensor(out=steps(arg[:, half, 1, :]), in0=k, scalar=vec[:, 1:2],
                                       in1=steps(tau[:, half, :]), op0=ALU.add, op1=ALU.subtract
                                       ).then_inc(s["new_u_arg_ready"], 1)
                v.wait_ge(s["proj_ready"], 3 * half + 3)
                v.wait_ge(s["back_sb"], 3 * half + 3)
                v.tensor_tensor(rec[:, half, :], ps[4 * half + 3][:], back[:, half, 2, :], ALU.mult
                                ).then_inc(s["r_ready"], 1)
                v.tensor_tensor(val[:, half, :], ps[4 * half + 2][:], back[:, half, 1, :], ALU.mult
                                ).then_inc(s["val_ready"], 1)
            per_half(wkv_args)

            def wkv_sums(half):
                flat = "p b t -> p (b t)"
                v.wait_ge(s["new_ready"], half + 1)
                v.wait_ge(s["dec_ready"], half + 1)
                got_beta = note(v.tensor_tensor_scan(
                    beta[:, half].rearrange(flat), dec_pad[:, half].rearrange(flat),
                    new_pad[:, half].rearrange(flat), 0.0, ALU.mult, ALU.add))
                v.wait_ge(s["newv_ready"], half + 1)
                v.tensor_tensor_scan(
                    alpha[:, half].rearrange(flat), dec_pad[:, half].rearrange(flat),
                    newv_pad[:, half].rearrange(flat), 0.0, ALU.mult, ALU.add
                    ).then_inc(s["alpha_ready"], 1)
                v.wait_ge(s["e1_ready"], half + 1)
                v.wait_ge(s["e2_ready"], half + 1)
                pr = prod[:, half]
                e1, e2 = e12[:, half, 0, :], e12[:, half, 1, :]
                v.wait_ge(s["vec_step"], got_beta)
                then(v.tensor_tensor(steps(pr[:, 0, :]), steps(e1), beta[:, half, :, 0:T], ALU.mult))
                weight = note(v.tensor_tensor(pr[:, 0, :], pr[:, 0, :], e2, ALU.add))
                v.wait_ge(s["vec_step"], weight)
                v.wait_ge(s["exp_r_ready"], half + 1)
                return note(v.scalar_tensor_tensor(out=pr[:, 3, :], in0=exp_r[:, half, :], scalar=1.0,
                                                   in1=pr[:, 0, :], op0=ALU.add, op1=ALU.mult))

            def wkv_quotient(half, divisor):
                pr = prod[:, half]
                v.wait_ge(s["vec_step"], divisor)
                then(v.reciprocal(pr[:, 0, :], pr[:, 3, :]))
                v.wait_ge(s["numerator_ready"], half + 1)
                v.tensor_tensor(mixed_o[:, half, :], pr[:, 1, :], pr[:, 0, :], ALU.mult
                                ).then_inc(s["o_ready"], 1)

            def mean_squares_o(half):
                mean_squares(half, HT, (s["sumsq_o"], ps[4 * half][:, 0:HT]), s["meansq_o"])

            def scale_rows_o(half):
                scale_rows(half, HT, s["rms_o"], w_back[:, 3:4].unsqueeze(2).broadcast_to([P, 1, HT]),
                           s["scale_o"])

            def quantise_o(half):
                v.wait_ge(s["bc_o"], half + 1)
                then(v.tensor_tensor(scaled[:, half, 0, :], weighted[:, half, 0, :],
                                     ps[4 * half + 2][:], ALU.mult))
                v.tensor_scalar(quant[:, half, 0, :], scaled[:, half, 0, :], ROUND, -ROUND,
                                ALU.add, ALU.add).then_inc(s["quant_o"], 1)

            def residual(half):
                v.wait_ge(s["out_ps"], half + 1)
                v.wait_ge(s["in_x"], 16)
                for n in range(HT):
                    t = half * HT + n
                    last = v.scalar_tensor_tensor(out=x2[:, t, :], in0=ps[4 * half + 3][:, n * D:(n + 1) * D],
                                                  scalar=stat[:, half, 7, n:n + 1], in1=x_tok[:, t, :],
                                                  op0=ALU.mult, op1=ALU.add)
                last.then_inc(s["x2_ready"], 1)

            wkv_quotient(0, wkv_sums(0))
            divisor = wkv_sums(1)
            mean_squares_o(0)
            peaks(0, HT, s["wo_t"])
            scale_rows_o(0)
            wkv_quotient(1, divisor)
            quantise_o(0)
            residual(0)
            mean_squares_o(1)
            peaks(1, HT, s["wo_t"])
            scale_rows_o(1)
            quantise_o(1)
            v.wait_ge(s["penalty_ready"], 1)
            v.tensor_reduce(count[:], mask[:], AX_X, ALU.add).then_inc(s["count_ready"], 1)

            def soft_in(half):
                v.wait_ge(s["score_ps"], half + 1)
                for g in range(4):
                    r = slice(32 * g, 32 * g + 32)
                    last = v.tensor_tensor(scores[r, half], tiles(ps[4 * half][:])[r, :, 32 * g:32 * g + 32],
                                           penalty[r, half * HT:(half + 1) * HT, :], ALU.add)
                then(last)
                then(v.tensor_reduce(row[:, half, 0, :], scores[:, half], AX_X, ALU.max))
                v.tensor_tensor(scores[:, half], scores[:, half],
                                row[:, half, 0, :].unsqueeze(2).broadcast_to([P, HT, T]), ALU.subtract
                                ).then_inc(s["soft_arg"], 1)

            def soft_out(half):
                v.wait_ge(s["exp_s"], half + 1)
                v.wait_ge(s["count_ready"], 1)
                then(v.tensor_reduce(row[:, half, 1, :], soft[:, half], AX_X, ALU.add))
                then(v.tensor_tensor(row[:, half, 2, :], row[:, half, 1, :],
                                     count[:, half * HT:(half + 1) * HT], ALU.mult))
                then(v.reciprocal(row[:, half, 3, :], row[:, half, 2, :]))
                then(v.tensor_tensor(soft_n[:, half], soft[:, half],
                                     row[:, half, 3, :].unsqueeze(2).broadcast_to([P, HT, T]), ALU.mult))
                for g in range(4):
                    r = slice(32 * g, 32 * g + 32)
                    last = v.transpose(blocks[r, half, :, 32 * g:32 * g + 32], soft_n[r, half])
                last.then_inc(s["blocks_ready"], 1)

            residual(1)
            for half in range(HALVES):
                soft_in(half)
                soft_out(half)

            def y_low(half):
                v.wait_ge(s["y_hi_ready"], half + 1)
                v.tensor_tensor(y_lo[:, half, :], y[:, half, :], y_hi[:, half, :].bitcast(F32),
                                ALU.subtract).then_inc(s["y_split"], 1)
            per_half(y_low)
            wide = [P, TILES, E_ROUTED]
            ge, gt = gate_e, gate_t

            def over(k):
                return gt[:, k, :].unsqueeze(2).broadcast_to(wide)
            rk = rank[:].unsqueeze(1).broadcast_to(wide)
            v.wait_ge(s["logit_ps"], 2)
            v.wait_ge(s["y_hi_ready"], 3)
            v.tensor_tensor(ge[:, 0], bc_ps[0][:, 0:TILES * E_ROUTED].rearrange("p (n e) -> p n e", n=TILES),
                            rbias[:].unsqueeze(1).broadcast_to(wide), ALU.mult
                            ).then_inc(s["yw_ready"], 2)
            v.tensor_tensor(yw_lo[1][:], y[:, 1, :], yw_hi[1][:].bitcast(F32), ALU.subtract
                            ).then_inc(s["yw_split"], 1)
            v.wait_ge(s["exp_l"], 1)
            then(v.tensor_scalar(ge[:, 2], ge[:, 1], 1.0, None, ALU.add))
            then(v.reciprocal(ge[:, 3], ge[:, 2]))

            def largest(k, probs):
                then(v.tensor_reduce(gt[:, k, :], ge[:, probs], AX_X, ALU.max))
                then(v.tensor_tensor(ge[:, 4], ge[:, probs], over(k), ALU.is_equal))
                then(v.tensor_tensor(ge[:, 4], ge[:, 4], rk, ALU.mult))
                then(v.tensor_reduce(gt[:, 2 + k, :], ge[:, 4], AX_X, ALU.max))
                then(v.tensor_tensor(ge[:, 5 + 2 * k], rk, over(2 + k), ALU.is_equal))

            def route_weights():
                then(v.tensor_tensor(gt[:, 4, :], gt[:, 0, :], gt[:, 1, :], ALU.add))
                then(v.reciprocal(gt[:, 5, :], gt[:, 4, :]))
                v.tensor_tensor(gt[:, 6, :], gt[:, 0, :], gt[:, 5, :], ALU.mult)
                then(v.tensor_tensor(gt[:, 7, :], gt[:, 1, :], gt[:, 5, :], ALU.mult))
                v.tensor_tensor(ge[:, 5], ge[:, 5], over(6), ALU.mult)
                then(v.tensor_tensor(ge[:, 7], ge[:, 7], over(7), ALU.mult))
                v.tensor_tensor(route[:], ge[:, 5], ge[:, 7], ALU.add).then_inc(s["route_ready"], 1)
                v.wait_ge(s["route_ready"], 1)

            def yw_product(n, b):
                v.wait_ge(s["bc_ready"], n - 1)
                v.wait_ge(s["yw_split"], n - 1)
                v.tensor_tensor(yw, y[:, b, :], bc_ps[b][:], ALU.mult).then_inc(s["yw_ready"], 1)

            def yw_low(n, b):
                v.wait_ge(s["yw_hi_ready"], n - 1)
                v.tensor_tensor(yw_lo[b][:], yw, yw_hi[b][:].bitcast(F32), ALU.subtract
                                ).then_inc(s["yw_split"], 1)

            def product(q, b, c):
                rows = CH[c][1]
                v.wait_ge(s["silu_ready"], q + 1)
                if not isinstance(q, int) or q > 1:
                    v.wait_ge(s["hid_split"], q - 1)
                v.tensor_tensor(hid[0:rows, b, :], silu[0:rows, b, :], up_ps[b][0:rows, :], ALU.mult
                                ).then_inc(s["hid_ready"], 1)

            def low(q, b, c):
                rows = CH[c][1]
                v.wait_ge(s["hid_hi_ready"], q + 1)
                v.tensor_tensor(hid_lo[c][0:rows, :], hid[0:rows, b, :],
                                hid_hi[c][0:rows, :].bitcast(F32), ALU.subtract
                                ).then_inc(s["hid_split"], 1)

            def column(e, half):
                v.tensor_copy(route_col[:, half, :].unsqueeze(2),
                              route[:, half * HT:(half + 1) * HT, bass.ds(e - 1, 1)]
                              ).then_inc(s["column_ready"], 1)

            largest(0, 3)
            then(v.scalar_tensor_tensor(out=ge[:, 6], in0=ge[:, 5], scalar=-2.0, in1=ge[:, 3],
                                        op0=ALU.mult, op1=ALU.add))
            product(0, 0, 0)
            largest(1, 6)
            product(1, 1, 1)
            low(0, 0, 0)
            route_weights()
            column(1, 0)
            product(2, 0, 2)
            low(1, 1, 1)

            def body(i, last):
                for u in range(4):
                    for c in range(NCH):
                        k = NCH * u + c
                        if not (last and u == 3):
                            product(i * (4 * NCH) + (k + 3), (k + 3) % 2, c)
                        if c == 0 and not (last and u >= 2):
                            yw_product(i * 4 + (u + 2), u % 2)
                            if not (last and u >= 1):
                                column(i * 2 + (u + 3) // 2, (u + 3) % 2)
                        if c == 1 and not (last and u >= 2):
                            yw_low(i * 4 + (u + 2), u % 2)
                        if not (last and u == 3 and c > 0):
                            low(i * (4 * NCH) + (k + 2), k % 2, (c + 2) % NCH)

            with v.Fori(0, E_ALL // 2 - 1) as i:
                body(i, False)
            body(E_ALL // 2 - 1, True)
            for half in range(HALVES):
                v.wait_ge(s["out_t"], half + 1)
                v.tensor_tensor(final[:, half * HT:(half + 1) * HT, :], tiles(ps[half][:]),
                                x2[:, half * HT:(half + 1) * HT, :], ALU.add
                                ).then_inc(s["out_ready"], 1)

        @block.tensor
        def _(pe):
            def per_half(f):
                for half in range(HALVES):
                    f(half)

            def spread(bank, column):
                for n in range(HT):
                    last = pe.transpose(bank[:, n * P:(n + 1) * P], lane(column(n), P), ident[:])
                return last

            def keep_warm(bank, count):
                for _ in range(count):
                    pe.matmul(bank[:], zeros[:, 0:P], zeros[:], start=True, stop=True)

            pe.wait_ge(s["zeros_ready"], 1)
            keep_warm(ps[6], 15)
            def cond_product(half):
                pe.wait_ge(in_xt[half], 16)
                for k, (first, end) in GATHER.items():
                    pe.wait_ge(gathered[k], (half + 1) * (end - first))
                for j in reversed(range(HB)):
                    b, j0 = half * HB + j, max(0, j + 1 - WIDE // T)
                    last = pe.matmul(ps[4 * half][:, j0 * T:(j + 1) * T], cond_w[:, b, 0:D],
                                     x_ch[:, half * HB + j0:b + 1, :], start=True, stop=True)
                last.then_inc(s["h_ps"], 1)
            cond_product(0)
            pe.wait_ge(s["abs_ready"], 1)
            pe.wait_ge(s["const_ready"], 10)
            pe.matmul(ps[7][:, 0:4], ones[:], abs_sum[:], start=True, stop=True).then_inc(s["tot_ready"], 1)
            cond_product(1)
            pe.wait_ge(s["ident_ready"], 1)

            def sum_squares(bank, column, squares):
                for n in range(HT):
                    at = column + n
                    last = pe.matmul(bank[:, at:at + WIDE], squares[:, n * P:(n + 1) * P],
                                     ones[:, 0:WIDE], start=True, stop=True)
                return last

            def turn(half):
                for m in range(3):
                    pe.wait_ge(s["square_ready"], 3 * half + m + 1)
                    last = sum_squares(ps[4 * half], m * HT, square[:, half, m, :])
                    if m == 2:
                        last.then_inc(s["sumsq_ready"], 1)
                    pe.wait_ge(*((s["weighted_ready"], 2 * half + m + 1) if m < 2 else
                                 (s["weighted_r"], half + 1)))
                    for n in range(HT):
                        last = pe.transpose(ps[4 * half + 1 + m][:, n * P:(n + 1) * P],
                                            weighted[:, half, m, n * P:(n + 1) * P], ident[:])
                    last.then_inc(s["weighted_t"], 1)
            turn(0)
            pe.wait_ge(s["w_mean_ready"], 1)
            turn(1)
            pe.wait_ge(s["meansq_ready"], 1)
            keep_warm(ps[0], 8)

            def scale_out(half):
                pe.wait_ge(s["scale_ready"], 2 * half + 2)
                for m in range(3):
                    spread(ps[4 * half + 1 + m],
                           lambda n: stat[:, half, 6, m * HT + n:m * HT + n + 1]
                           ).then_inc(s["scale_bc"], 1)
            per_half(scale_out)

            def project(half):
                pe.wait_ge(s["w_q_ready"], 1)
                for m in range(3):
                    if m:
                        pe.wait_ge(s["back_sb"], 3 * half + m)
                    spread(ps[4 * half], lambda n: stat[:, half, 7, m * HT + n:m * HT + n + 1]
                           ).then_inc(s["back_bc"], 1)
                    pe.wait_ge(s["quant_ready"], 3 * half + m + 1)
                    pe.matmul(ps[4 * half + 1 + m][:], w_q[:, m, :], quant[:, half, m, :],
                              start=True, stop=True).then_inc(s["proj_ready"], 1)
            per_half(project)

            def turn_o(half):
                pe.wait_ge(s["sq_o"], half + 1)
                sum_squares(ps[4 * half], 0, square[:, half, 0, :]).then_inc(s["sumsq_o"], 1)
                pe.wait_ge(s["wo_ready"], half + 1)
                for n in range(HT):
                    last = pe.transpose(ps[4 * half + 1][:, n * P:(n + 1) * P],
                                        weighted[:, half, 0, n * P:(n + 1) * P], ident[:])
                last.then_inc(s["wo_t"], 1)

            def scale_out_o(half):
                pe.wait_ge(s["scale_o"], 2 * half + 2)
                spread(ps[4 * half + 2], lambda n: stat[:, half, 6, n:n + 1]).then_inc(s["bc_o"], 1)

            def project_o(half):
                pe.wait_ge(s["quant_o"], half + 1)
                for n in range(HT):
                    last = pe.matmul(ps[4 * half + 3][:, n * D:(n + 1) * D],
                                     quant[:, half, 0, n * P:(n + 1) * P], w_q[:, 3, :],
                                     start=True, stop=True)
                last.then_inc(s["out_ps"], 1)

            def x2_turn(half):
                pe.wait_ge(s["x2_ready"], half + 1)
                for n in range(HT):
                    last = pe.transpose(ps[4 * half + 1][:, n * P:(n + 1) * P], x2[:, half * HT + n, :],
                                        ident[:])
                last.then_inc(s["x2_t_ps"], 1)
            def score(half):
                pe.wait_ge(s["in_small"], 64)
                pe.wait_ge(s["x2_t_ready"], half + 1)
                pe.matmul(ps[4 * half + 2][0:A_DIM, :], w1_sb[:], x2_t[:, half, :], start=True, stop=True
                          ).then_inc(s["w1_ps"], 1)

            def score_rows(half):
                pe.wait_ge(s["tanh_ready"], half + 1)
                pe.matmul(ps[4 * half][:], b1v[:, 1:2].broadcast_to([A_DIM, P]), tanh_t[:, half, :],
                          start=True, stop=True).then_inc(s["score_ps"], 1)

            def pooled(half):
                pe.wait_ge(s["blocks_ready"], half + 1)
                for n in range(HT):
                    last = pe.matmul(ps[4 * half + 1][:, n * P:(n + 1) * P], x2[:, half * HT + n, :],
                                     blocks[:, half, n, :], start=True, stop=True)
                last.then_inc(s["pooled_ps"], 1)

            turn_o(0)
            scale_out_o(0)
            keep_warm(ps[7], 8)
            project_o(0)
            turn_o(1)
            x2_turn(0)
            score(0)
            scale_out_o(1)
            keep_warm(ps[7], 5)
            project_o(1)
            score_rows(0)
            keep_warm(ps[6], 2)
            x2_turn(1)
            keep_warm(ps[6], 3)
            score(1)
            keep_warm(ps[4], 4)
            score_rows(1)
            pooled(0)
            keep_warm(ps[6], 4)
            for half in range(HALVES):
                pe.matmul(acc_ps[half][:], zeros[:, 0:P], zeros[:], start=True, stop=False,
                          skip_group_check=True)
            pooled(1)

            def logits(half):
                pe.wait_ge(s["y_ready"], half + 1)
                if half == 0:
                    pe.wait_ge(s["soft_arg"], 2)
                for n in range(HT):
                    at = (half * HT + n) * E_ROUTED
                    last = pe.matmul(ps[4][:, at:at + WIDE], y[:, half, n * P:(n + 1) * P], wr[:],
                                     start=True, stop=True)
                last.then_inc(s["logit_ps"], 1)
            per_half(logits)

            def spread_route(n, half):
                pe.wait_ge(s["column_ready"], n - 1)
                spread(bc_ps[half], lambda t: route_col[:, half, t:t + 1]).then_inc(s["bc_ready"], 1)

            def three(bank, lhs, rhs, start, stop):
                for k, (a, b) in enumerate(((0, 0), (0, 1), (1, 0))):
                    last = pe.matmul(bank, lhs[a], rhs[b], start=start and k == 0, stop=stop and k == 2,
                                     skip_group_check=not start)
                return last

            def gate_up(buf, w, half, c, up_in):
                at, rows = CH[c]
                three(gate_ps[buf][0:rows, :], (w_hi[w][:, at:at + rows], w_lo[w][:, at:at + rows]),
                      (y_hi[:, half, :], y_lo[:, half, :]), True, True)
                at += HID
                three(up_ps[buf][0:rows, :], (w_hi[w][:, at:at + rows], w_lo[w][:, at:at + rows]),
                      up_in, True, True).then_inc(s["gu_ready"], 1)

            def down(w, half, c, stop):
                rows = CH[c][1]
                at = GU + c * D
                return three(acc_ps[half][:], (w_hi[w][0:rows, at:at + D], w_lo[w][0:rows, at:at + D]),
                             (hid_hi[c][0:rows, :], hid_lo[c][0:rows, :]), False, stop)

            pe.wait_ge(s["y_split"], 1)
            pe.wait_ge(s["weight_split"], 1)
            for c in range(NCH):
                if c == 2:
                    pe.wait_ge(s["hid_ready"], 1)
                gate_up(c % 2, 0, 0, c, (y_hi[:, 0, :], y_lo[:, 0, :]))

            def body(i, last_body):
                for u in range(4):
                    w, half = u // 2, u % 2
                    final_unit = last_body and u == 3
                    nw, nhalf = ((u + 1) // 2) % 2, (u + 1) % 2
                    for c in range(NCH):
                        q = NCH * u + c
                        if not final_unit:
                            if c == 0:
                                pe.wait_ge(s["weight_split"], i * 2 + ((u + 1) // 2 + 1))
                                pe.wait_ge(s["yw_split"], i * 4 + (u + 1))
                            pe.wait_ge(s["hid_ready"], i * (4 * NCH) + (q + 2))
                            gate_up((q + 3) % 2, nw, nhalf, c, (yw_hi[nhalf][:], yw_lo[nhalf][:]))
                        if c == 0 and not (last_body and u >= 2):
                            pe.wait_ge(s["yw_ready"], i * 4 + (u + 1))
                            spread_route(i * 4 + (u + 2), u % 2)
                        pe.wait_ge(s["hid_split"], i * (4 * NCH) + (q + 1))
                        done = last_body and u >= 2 and c == NCH - 1
                        last = down(w, half, c, done)
                        if u % 2 == 1 and c == NCH - 1:
                            last.then_inc(s["expert_used"], 1)
                        elif done:
                            last.then_inc(s["acc_ready"], 1)

            with pe.Fori(0, E_ALL // 2 - 1) as i:
                body(i, False)
            body(E_ALL // 2 - 1, True)

            def out_turn(half):
                pe.wait_ge(s["acc_out"], half + 1)
                for n in range(HT):
                    last = pe.transpose(ps[half][:, n * P:(n + 1) * P], acc_sb[:, half, n * P:(n + 1) * P],
                                        ident[:])
                last.then_inc(s["out_t"], 1)
            per_half(out_turn)


def kernel(**inputs):
    import numpy as np
    import concourse.bacc as bacc
    from concourse.bass_utils import run_bass_kernel_spmd as run

    a = {k: np.asarray(v) for k, v in inputs.items()}
    attn = [a["L0_attn_" + n] for n in ("w_key", "w_value", "w_receptance", "w_output")]

    def experts_of(kind):
        return np.concatenate([a["L0_ffn_shared_" + kind][None], a["L0_ffn_routed_" + kind]])

    down = experts_of("down")
    padded = np.zeros((E_ALL, NCH * P, D), down.dtype)
    padded[:, :HID] = down
    arrays = {
        "x": a["x"],
        "x_t": a["x"].reshape(B * T, D).T,
        "subject": a["itok_B_0_15"].reshape(1, B),
        "prompt_type": a["itok_B_0_2"].reshape(TILES, 4).T,
        "cond": np.concatenate([a["L0_cond_weights"], a["L0_cond_b"][:, :, None]], axis=2
                               ).transpose(1, 0, 2).reshape(D, SUBJECTS * (D + 1)),
        "cols": np.stack([a["L0_attn_" + n].reshape(D) for n in (
            "time_decay", "time_first", "time_mix_key", "time_mix_value", "time_mix_receptance",
            "rms_key", "rms_value", "rms_receptance", "rms_output")], axis=1),
        "attn_w": np.concatenate([w.T for w in attn], axis=1),
        "w1": a["L0_cond2_W1"],
        "b1_v": np.stack([a["L0_cond2_b1"], a["L0_cond2_v"]], axis=1),
        "router_w": a["L0_ffn_Wr"],
        "router_b": a["L0_ffn_routing_bias"].reshape(1, E_ROUTED),
        "experts": np.concatenate(
            [experts_of("gate"), experts_of("up"),
             padded.reshape(E_ALL, NCH, P, D).transpose(0, 2, 1, 3).reshape(E_ALL, P, NCH * D)], axis=2),
    }
    nc = bacc.Bacc("TRN2", target_bir_lowering=False, num_devices=1)
    feed, args = {}, []
    for name, value in arrays.items():
        value = np.ascontiguousarray(value)
        feed["in_" + name] = value
        args.append(nc.dram_tensor("in_" + name, value.shape, mybir.dt.from_np(value.dtype),
                                   kind="ExternalInput").ap())
    out = nc.dram_tensor("out_0", (B, T, D), F32, kind="ExternalOutput").ap()
    adaln_attention_ffn(nc, *args, out)
    return run(nc, [feed], core_ids=[0]).results[0]["out_0"]
```

```python
from contextlib import ExitStack

import concourse.bass as bass
from concourse import mybir

ALU = mybir.AluOpType
ACT = mybir.ActivationFunctionType
AX_X = mybir.AxisListType.X
F32 = mybir.dt.float32
F32R = mybir.dt.float32r
BF16 = mybir.dt.bfloat16
I32 = mybir.dt.int32

P = 128
B, T, D = 32, 32, 128
SUBJECTS = 16
GATHER = {"vector": (0, 7), "scalar": (7, 14), "gpsimd": (14, 16)}
TILES = B * T // P
HALVES = 2
HB = B // HALVES
HT = TILES // HALVES
N = HB * T
TP = T + 1
HID = 352
E_ROUTED = 7
E_ALL = E_ROUTED + 1
A_DIM = 32
QROWS = 32
QUARTERS = P // QROWS
PER_EXPERT = HID // QROWS
CHUNKS = E_ALL * PER_EXPERT // QUARTERS
PLAIN = 2
BODY = 4
TURNS = (CHUNKS - PLAIN) // BODY
BODY_STEPS = HALVES * BODY
STEPS = HALVES * CHUNKS
SPREADS = BODY_STEPS - HALVES
LAG = 3
HID_BUFS = 4
CHUNK_W = 3 * P
PACK = 2 * CHUNK_W
PARTS = [slice(0, N // 2), slice(N // 2, N)]
LO = 32
ROUND = 12582912.0
RMS_EPS = 1e-8
TINY = 1e-5
WIDE = 128
BIG = 1e30
NEAR_ZERO = 1e-20
COL = {n: i for i, n in enumerate(
    ["decay", "first", "mix_k", "mix_v", "mix_r", "rms_k", "rms_v", "rms_r", "rms_o"])}


def adaln_attention_ffn(nc, x, x_t, subject, prompt_type, cond, cols, attn_w, w1, b1_v,
                        router_w, router_b, quarter_owner, experts, out):
    ctx = ExitStack()
    with ctx:
        def sb(name, shape, dt=F32):
            return ctx.enter_context(nc.sbuf_tensor(name, shape, dt))

        def sem(name):
            return ctx.enter_context(nc.semaphore(name))

        x_tok = sb("x_tok", [P, TILES, D])
        x_ch = sb("x_ch", [P, B, T])
        subj = sb("subj", [1, B], I32)
        ptype_i = sb("ptype_i", [P, TILES], I32)
        cond_w = sb("cond_w", [P, B, D + 1])
        vec = sb("vec", [P, len(COL)])
        aw = sb("aw", [P, 4, D])
        w1_sb = sb("w1_sb", [P, A_DIM])
        b1v = sb("b1v", [A_DIM, 2])
        wr = sb("wr", [P, WIDE])
        rbias = sb("rbias", [P, E_ROUTED])
        owner_in = sb("owner_in", [LO + E_ALL, (CHUNKS - PLAIN) * QUARTERS])
        staging = sb("staging", [P, SUBJECTS * (D + 1)])
        raw = staging[:, 0:2 * PACK].rearrange("p (b n) -> p b n", b=2)
        cond_all = staging[:].rearrange("p (s d) -> p s d", s=SUBJECTS)

        ident = sb("ident", [P, P])
        ones = sb("ones", [P, P])
        zeros = sb("zeros", [P, N], BF16)
        zero_col = sb("zero_col", [P, 1])
        neg_half = sb("neg_half", [P, 3 * HT])
        diff = sb("diff", [P, T])
        below = sb("below", [P, T])
        above = sb("above", [P, T])
        other = sb("other", [P, T])
        ptype = sb("ptype", [P, TILES])
        is_kind = sb("is_kind", [P, 3, TILES])
        mask = sb("mask", [P, TILES, T])
        mask_b = sb("mask_b", [P, TILES, T])
        penalty = sb("penalty", [P, TILES, T])
        count = sb("count", [P, TILES])
        rank = sb("rank", [P, E_ROUTED])
        one_less = sb("one_less", [P, 3])
        decay = sb("decay", [P, 1])
        log_w = sb("log_w", [P, 1])
        scan_w = sb("scan_w", [P, HB, TP])

        abs_sum = sb("abs_sum", [P, 4])
        w_mean = sb("w_mean", [P, 4])
        w_scale = sb("w_scale", [P, 4])
        w_back = sb("w_back", [P, 4])
        w_q = sb("w_q", [P, 4, D], BF16)

        h_pad = sb("h_pad", [P, HALVES, HB, TP])
        shifted = sb("shifted", [P, HALVES, 3, N])
        mixed = sb("mixed", [P, HALVES, 3, N])
        square = sb("square", [P, HALVES, 3, N])
        weighted = sb("weighted", [P, HALVES, 3, N])
        scaled = mixed
        quant = sb("quant", [P, HALVES, 3, N], BF16)
        stat = sb("stat", [P, HALVES, 8, 3 * HT])
        back = square
        k_pad = sb("k_pad", [P, HALVES, HB, TP])
        val, rec, exp_r = (shifted[:, :, m, :] for m in range(3))
        eps = sb("eps", [P, HALVES, HB, TP])
        dec_arg, new_arg = weighted[:, :, 1, :], weighted[:, :, 2, :]
        dec_pad = sb("dec_pad", [P, HALVES, HB, TP])
        new_pad = sb("new_pad", [P, HALVES, HB, TP])
        newv_pad = sb("newv_pad", [P, HALVES, HB, TP])
        alpha = sb("alpha", [P, HALVES, HB, TP])
        beta = sb("beta", [P, HALVES, HB, TP])
        lead, arg = mixed[:, :, 0, :], mixed[:, :, 1:3, :]
        e12 = sb("e12", [P, HALVES, 2, N])
        w_round, w_clip = (e12[:, k, 0, :].rearrange("p (m d) -> p m d", m=4) for k in range(2))
        prod = cond_w[:].rearrange("p b d -> p (b d)")[:, 0:HALVES * 4 * N].rearrange(
            "p (h k n) -> p h k n", h=HALVES, k=4)
        mixed_o = weighted[:, :, 2, :]
        x2 = sb("x2", [P, TILES, D])
        x2_t = weighted[:, :, 1, :]
        tanh_t = prod[0:A_DIM, 0, 0:HALVES, :]
        scores = sb("scores", [P, HALVES, HT, T])
        soft = sb("soft", [P, HALVES, HT, T])
        soft_n = sb("soft_n", [P, HALVES, HT, T])
        row = sb("row", [P, HALVES, 4, HT])
        blocks = sb("blocks", [P, HALVES, HT, P])
        y = x_ch[:].rearrange("p (h b) t -> p h (b t)", h=HALVES)
        y_hi = sb("y_hi", [P, HALVES, N], F32R)
        y_lo = sb("y_lo", [P, HALVES, N], F32R)
        gate_e = sb("gate_e", [P, 8, TILES, E_ROUTED])
        gate_t = sb("gate_t", [P, 8, TILES])
        route = sb("route", [P, TILES, LO + E_ALL], F32R)
        route_t = sb("route_t", [LO + E_ALL, HALVES, N], F32R)
        owner = sb("owner", [LO + E_ALL, BODY, P], F32R)

        w_hi = [sb(f"w_hi{i}", [P, CHUNK_W], F32R) for i in range(BODY)]
        w_lo = [sb(f"w_lo{i}", [P, CHUNK_W], F32R) for i in range(BODY)]
        silu, hid = mixed[:, 0, 0:2, :], mixed[:, 1, 0:2, :]
        hid_hi = [sb(f"hid_hi{i}", [P, N], F32R) for i in range(HID_BUFS)]
        hid_lo = [sb(f"hid_lo{i}", [P, N], F32R) for i in range(HID_BUFS)]
        acc_sb = square[:, :, 0, :]
        final = weighted[:].rearrange("p h m n -> p (h m n)")[:, 0:TILES * D].rearrange(
            "p (n d) -> p n d", n=TILES)

        ps = [ctx.enter_context(nc.psum_tensor(f"ps{i}", [P, 512], F32)) for i in range(8)]
        gate_ps, up_ps, bc_ps, acc_ps = ps[0:2], ps[2:4], ps[4:6], ps[6:8]

        def tiles(ap):
            return ap.rearrange("p (n c) -> p n c", n=HT)

        def steps(ap):
            return ap.rearrange("p (b t) -> p b t", t=T)

        def lane(ap, n):
            return ap.broadcast_to([P, n])

        names = """in_subj in_vec in_aw in_small in_x in_type in_cond stored
            const_ready zeros_ready zero_ready ident_ready one_less_done decay_done log_w_ready scan_ready abs_ready
            tot_ready w_mean_ready w_q_ready back_ready penalty_ready count_ready
            h_ps h_ready shift_ready mix_ready square_ready weighted_ready weighted_vr weighted_t sumsq_ready
            meansq_ready rms_ready scale_ready scale_bc quant_ready proj_ready back_bc back_sb
            k_ready eps_ready val_ready newv_ready e2v_ready r_ready exp_r_ready dec_arg_ready new_arg_ready dec_ready new_ready
            old_arg_ready new_u_arg_ready e1_ready e2_ready lead_ready alpha_ready old_v_ready numerator_ready o_ready sq_o wo_ready wo_t sumsq_o meansq_o rms_o scale_o
            bc_o quant_o out_ps x2_ready x2_t_ps x2_t_ready w1_ps tanh_ready score_ps
            soft_arg exp_s blocks_ready pooled_ps y_ready y_hi_ready y_split logit_ps
            silu_l route_ready vec_step pool_step pool_in
            weight_split weight_used in_owner owner_ready one_ready logit_in route_t_ps route_t_ready
            bc_ready bc_used gu_ready silu_ready hid_ready hid_hi_ready hid_split acc_ready acc_out last_down out_t out_ready""".split()
        s = {n: sem(n) for n in names}

        gathered = {k: sem("gathered_" + k) for k in GATHER}
        table = "a subject's number is a row of the table of subjects"

        def gather(name, engine, eng, copy):
            first, end = GATHER[name]
            eng.wait_ge(s["in_subj"], 16)
            who = [nc.values_load_multi_w_load_instructions(
                subj[0:1, half * HB + first:half * HB + end], engines=[engine], min_val=0,
                max_val=SUBJECTS - 1, skip_runtime_bounds_check_because=table)[1]
                for half in range(HALVES)]
            eng.wait_ge(s["in_cond"], 16)
            for half in range(HALVES):
                for k in range(end - first):
                    b = half * HB + first + k
                    copy(cond_w[:, b:b + 1, :], cond_all[:, bass.ds(who[half][k], 1), :]
                         ).then_inc(gathered[name], 1)

        in_xt = [sem(f"in_xt{h}") for h in range(HALVES)]
        expert_in = [sem(f"expert_in{b}") for b in range(2)]

        block = ctx.enter_context(nc.Block())

        @block.sync
        def _(sp):
            sp.dma_start(subj[:], subject).then_inc(s["in_subj"], 16)
            sp.dma_start(cond_all[:].rearrange("p s d -> p (s d)"), cond).then_inc(s["in_cond"], 16)
            x_half = x_ch[:].rearrange("p (h b) t -> p h (b t)", h=HALVES)
            sp.dma_start(x_half[:, 0, :], x_t[:, 0:N]).then_inc(in_xt[0], 16)
            sp.dma_start(aw[:].rearrange("p m d -> p (m d)"), attn_w).then_inc(s["in_aw"], 16)
            sp.dma_start(x_half[:, 1, :], x_t[:, N:]).then_inc(in_xt[1], 16)
            for g in range(4):
                sp.dma_start(ptype_i[32 * g:32 * g + 32, :],
                             prompt_type[g:g + 1, :].broadcast_to([32, TILES])
                             ).then_inc(s["in_type"], 16)
            sp.dma_start(x_tok[:], x.rearrange("b t d -> (b t) d").rearrange("(n p) d -> p n d", p=P)
                         ).then_inc(s["in_x"], 16)
            sp.dma_start(w1_sb[:], w1).then_inc(s["in_small"], 16)
            sp.dma_start(b1v[:], b1_v).then_inc(s["in_small"], 16)
            sp.dma_start(wr[:, 0:E_ROUTED], router_w).then_inc(s["in_small"], 16)
            sp.dma_start(owner_in[:], quarter_owner).then_inc(s["in_owner"], 16)
            sp.dma_start(rbias[:], router_b.broadcast_to([P, E_ROUTED])).then_inc(s["in_small"], 16)
            for k, (first, end) in GATHER.items():
                sp.wait_ge(gathered[k], HALVES * (end - first))
            for g in range(2):
                sp.dma_start(raw[:, g, :], experts[g]).then_inc(expert_in[g], 16)
            with sp.Fori(0, TURNS - 1) as i:
                for b in range(2):
                    sp.wait_ge(s["weight_split"], i * BODY + 2 * (b + 1))
                    sp.dma_start(raw[:, b, :], experts[bass.ds(i * 2 + (b + 2), 1)].rearrange(
                        "e p n -> p (e n)")).then_inc(expert_in[b], 16)
            sp.wait_ge(s["weight_split"], (TURNS - 1) * BODY + 2)
            sp.dma_start(raw[:, 0, :], experts[2 * TURNS]).then_inc(expert_in[0], 16)
            sp.wait_ge(s["out_ready"], 1)
            o_v = out.rearrange("b t d -> (b t) d").rearrange("(n p) d -> p n d", p=P)
            sp.dma_start(o_v[:, 0:HT, :], final[:, 0:HT, :]).then_inc(s["stored"], 16)
            sp.wait_ge(s["out_ready"], 2)
            sp.dma_start(o_v[:, HT:HT + HT // 2, :], final[:, HT:HT + HT // 2, :]).then_inc(s["stored"], 16)
            sp.wait_ge(s["out_ready"], 3)
            sp.dma_start(o_v[:, HT + HT // 2:, :], final[:, HT + HT // 2:, :]).then_inc(s["stored"], 16)
            sp.wait_ge(s["stored"], 48)

        @block.gpsimd
        def _(pool):
            step = [0]

            def then(ins):
                step[0] += 1
                ins.then_inc(s["pool_step"], 1)
                pool.wait_ge(s["pool_step"], step[0])

            pool.memset(zeros[:], 0.0).then_inc(s["zeros_ready"], 1)
            pool.memset(ident[:], 0.0).then_inc(s["zero_ready"], 1)
            pool.wait_ge(s["zero_ready"], 1)
            pool.affine_select(out=ident[:], in_=ident[:], compare_op=ALU.not_equal, fill=1.0, base=0,
                               pattern=[[-1, P]], channel_multiplier=1).then_inc(s["ident_ready"], 1)
            pool.memset(ones[:], 1.0).then_inc(s["const_ready"], 1)
            pool.memset(zero_col[:], 0.0).then_inc(s["const_ready"], 1)
            pool.memset(wr[:, E_ROUTED:], 0.0).then_inc(s["const_ready"], 1)
            pool.memset(neg_half[:], -0.5).then_inc(s["const_ready"], 1)
            pool.memset(h_pad[:, :, :, 0:1], 0.0).then_inc(s["const_ready"], 1)
            pool.memset(k_pad[:, :, :, 0:1], 0.0).then_inc(s["const_ready"], 1)
            pool.memset(dec_pad[:, :, :, 0:1], 0.0).then_inc(s["const_ready"], 1)
            pool.memset(new_pad[:, :, :, 0:1], 0.0).then_inc(s["const_ready"], 1)
            pool.memset(newv_pad[:, :, :, 0:1], 0.0).then_inc(s["const_ready"], 1)
            pool.memset(blocks[:], 0.0).then_inc(s["const_ready"], 1)
            pool.memset(route[:].bitcast(F32), 0.0).then_inc(s["zero_ready"], 1)
            pool.wait_ge(s["zero_ready"], 2)
            pool.memset(route[:, :, 0:1].bitcast(F32), 1.0).then_inc(s["one_ready"], 1)
            pool.wait_ge(s["const_ready"], 10)
            for g in range(4):
                then(pool.iota(diff[32 * g:32 * g + 32, :], pattern=[[1, T]], base=0,
                               channel_multiplier=-1, allow_small_or_imprecise_dtypes=True))
            then(pool.iota(rank[:], pattern=[[-1, E_ROUTED]], base=E_ROUTED, channel_multiplier=0,
                           allow_small_or_imprecise_dtypes=True))
            then(pool.tensor_scalar(below[:], diff[:], 0.0, None, ALU.is_le))
            then(pool.tensor_scalar(above[:], diff[:], 0.0, None, ALU.is_ge))
            then(pool.tensor_tensor(other[:], below[:], above[:], ALU.add))
            then(pool.tensor_scalar(other[:], other[:], -1.0, 2.0, ALU.mult, ALU.add))
            gather("gpsimd", mybir.EngineType.Pool, pool, pool.tensor_copy)
            pool.wait_ge(s["in_type"], 64)
            then(pool.tensor_copy(ptype[:], ptype_i[:]))
            then(pool.tensor_scalar(is_kind[:, 0, :], ptype[:], 0.0, None, ALU.is_equal))
            then(pool.tensor_scalar(is_kind[:, 1, :], ptype[:], 1.0, None, ALU.is_equal))
            then(pool.tensor_tensor(is_kind[:, 2, :], is_kind[:, 0, :], is_kind[:, 1, :], ALU.add))
            then(pool.tensor_scalar(is_kind[:, 2, :], is_kind[:, 2, :], -1.0, 1.0, ALU.mult, ALU.add))
            shape = [P, TILES, T]

            def term(dst, kind, rows):
                then(pool.tensor_tensor(dst[:], is_kind[:, kind, :].unsqueeze(2).broadcast_to(shape),
                                        rows[:].unsqueeze(1).broadcast_to(shape), ALU.mult))
            term(mask, 0, below)
            term(mask_b, 1, above)
            then(pool.tensor_tensor(mask[:], mask[:], mask_b[:], ALU.add))
            term(mask_b, 2, other)
            then(pool.tensor_tensor(mask[:], mask[:], mask_b[:], ALU.add))
            pool.tensor_scalar(penalty[:], mask[:], BIG, -BIG, ALU.mult, ALU.add
                               ).then_inc(s["penalty_ready"], 1)
            for half in range(HALVES):
                for m in (1, 2):
                    pool.wait_ge(s["mix_ready"], 3 * half + m + 1)
                    pool.tensor_tensor(weighted[:, half, m, :], mixed[:, half, m, :],
                                       vec[:, 5 + m:6 + m].broadcast_to([P, N]), ALU.mult
                                       ).then_inc(s["weighted_vr"], 1)
            for half in range(HALVES):
                pool.wait_ge(s["meansq_ready"], half + 1)
                pool.tensor_tensor(stat[:, half, 1, :], stat[:, half, 0, :], neg_half[:], ALU.pow
                                   ).then_inc(s["rms_ready"], 1)
            def minus(dst, a, b, done):
                pool.tensor_tensor(dst, a, b, ALU.subtract).then_inc(s[done], 1)

            def wkv_args(half):
                old, new = eps[:, half, :, 0:T], eps[:, half, :, 1:TP]
                pool.wait_ge(s["eps_ready"], half + 1)
                minus(steps(dec_arg[:, half, :]), old, new, "dec_arg_ready")
                minus(steps(new_arg[:, half, :]), k_pad[:, half, :, 1:TP], new, "new_arg_ready")
                pool.wait_ge(s["new_u_arg_ready"], half + 1)
                minus(arg[:, half, 0, :], arg[:, half, 1, :], lead[:, half, :], "old_arg_ready")

            def values(half):
                pool.wait_ge(s["new_ready"], half + 1)
                pool.wait_ge(s["val_ready"], half + 1)
                pool.tensor_tensor(newv_pad[:, half, :, 1:TP], new_pad[:, half, :, 1:TP],
                                   steps(val[:, half, :]), ALU.mult).then_inc(s["newv_ready"], 1)
                pool.wait_ge(s["e2_ready"], half + 1)
                pool.tensor_tensor(prod[:, half, 2, :], e12[:, half, 1, :], val[:, half, :], ALU.mult
                                   ).then_inc(s["e2v_ready"], 1)

            def numerator(half):
                pool.wait_ge(s["e1_ready"], half + 1)
                pool.wait_ge(s["alpha_ready"], half + 1)
                pool.tensor_tensor(steps(prod[:, half, 1, :]), steps(e12[:, half, 0, :]),
                                   alpha[:, half, :, 0:T], ALU.mult).then_inc(s["old_v_ready"], 1)
                pool.wait_ge(s["old_v_ready"], half + 1)
                pool.wait_ge(s["e2v_ready"], half + 1)
                pool.tensor_tensor(prod[:, half, 1, :], prod[:, half, 1, :], prod[:, half, 2, :],
                                   ALU.add).then_inc(s["numerator_ready"], 1)

            wkv_args(0)
            values(0)
            wkv_args(1)
            numerator(0)
            values(1)
            numerator(1)
            for half in range(HALVES):
                pool.wait_ge(s["meansq_o"], half + 1)
                pool.tensor_tensor(stat[:, half, 1, 0:HT], stat[:, half, 0, 0:HT], neg_half[:, 0:HT],
                                   ALU.pow).then_inc(s["rms_o"], 1)

            def own(at, k):
                pool.tensor_copy(owner[:, k, :].rearrange("e (q r) -> e q r", r=QROWS),
                                 owner_in[:, at].unsqueeze(2).broadcast_to(
                                     [LO + E_ALL, QUARTERS, QROWS])).then_inc(s["owner_ready"], 1)

            def split(c, k, load):
                b = (k // 2) % 2
                w = raw[:, b, (k % 2) * CHUNK_W:(k % 2 + 1) * CHUNK_W]
                pool.wait_ge(expert_in[b], load * 16)
                pool.tensor_tensor(w_hi[k][:], w, zero_col[:].broadcast_to([P, CHUNK_W]), ALU.add
                                   ).then_inc(s["pool_in"], 1)
                pool.wait_ge(s["pool_in"], c + 1)
                pool.tensor_tensor(w_lo[k][:], w, w_hi[k][:].bitcast(F32), ALU.subtract
                                   ).then_inc(s["weight_split"], 1)
            for c in range(BODY):
                split(c, c, 1)
                if c == PLAIN:
                    pool.wait_ge(s["in_owner"], 16)
                if c >= PLAIN:
                    own(slice((c - PLAIN) * QUARTERS, (c - PLAIN + 1) * QUARTERS), c)
            with pool.Fori(0, TURNS - 1) as i:
                for k in range(BODY):
                    pool.wait_ge(s["weight_used"], i * BODY + (k + 1))
                    split(i * BODY + (k + BODY), k, i + 2)
                    own(bass.ds(i * (BODY * QUARTERS) + (k + BODY - PLAIN) * QUARTERS, QUARTERS), k)
            for k in range(2):
                pool.wait_ge(s["weight_used"], (TURNS - 1) * BODY + (k + 1))
                split(TURNS * BODY + k, k, TURNS + 1)
                at = (TURNS * BODY + k - PLAIN) * QUARTERS
                own(slice(at, at + QUARTERS), k)

        @block.scalar
        def _(act):
            act.dma_start(vec[:], cols).then_inc(s["in_vec"], 16)
            act.wait_ge(s["in_vec"], 16)
            act.activation(decay[:], vec[:, 0:1], ACT.Exp).then_inc(s["decay_done"], 1)
            gather("scalar", mybir.EngineType.Activation, act,
                   lambda o, x: act.activation(o, x, ACT.Copy))

            def per_half(f):
                for half in range(HALVES):
                    f(half)

            def shift(half):
                act.wait_ge(s["h_ready"], half + 1)
                act.wait_ge(s["one_less_done"], 1)
                for m in range(3):
                    act.activation(steps(shifted[:, half, m, :]), h_pad[:, half, :, 0:T], ACT.Identity,
                                   scale=one_less[:, m:m + 1]).then_inc(s["shift_ready"], 1)

            def squares(half):
                for m in range(3):
                    act.wait_ge(s["mix_ready"], 3 * half + m + 1)
                    act.activation(square[:, half, m, :], mixed[:, half, m, :], ACT.Square
                                   ).then_inc(s["square_ready"], 1)
            for half in range(HALVES):
                shift(half)
                squares(half)

            def backs(half):
                for m in range(3):
                    act.wait_ge(s["back_bc"], 3 * half + m + 1)
                    act.activation(back[:, half, m, :], ps[4 * half][:], ACT.Copy
                                   ).then_inc(s["back_sb"], 1)
            per_half(backs)

            def exps(half):
                act.wait_ge(s["dec_arg_ready"], half + 1)
                act.activation(dec_pad[:, half, :, 1:TP], steps(dec_arg[:, half, :]), ACT.Exp,
                               bias=log_w[:, 0:1]).then_inc(s["dec_ready"], 1)
                act.wait_ge(s["new_arg_ready"], half + 1)
                act.activation(new_pad[:, half, :, 1:TP], steps(new_arg[:, half, :]), ACT.Exp
                               ).then_inc(s["new_ready"], 1)
                act.wait_ge(s["new_u_arg_ready"], half + 1)
                act.activation(e12[:, half, 1, :], arg[:, half, 1, :], ACT.Exp
                               ).then_inc(s["e2_ready"], 1)
                act.wait_ge(s["old_arg_ready"], half + 1)
                act.activation(e12[:, half, 0, :], arg[:, half, 0, :], ACT.Exp
                               ).then_inc(s["e1_ready"], 1)
                act.wait_ge(s["r_ready"], half + 1)
                act.activation(exp_r[:, half, :], rec[:, half, :], ACT.Exp, scale=-1.0
                               ).then_inc(s["exp_r_ready"], 1)
            per_half(exps)

            def weigh_o(half):
                act.wait_ge(s["o_ready"], half + 1)
                act.activation(square[:, half, 0, :], mixed_o[:, half, :], ACT.Square
                               ).then_inc(s["sq_o"], 1)
                act.activation(weighted[:, half, 0, :], mixed_o[:, half, :], ACT.Identity,
                               scale=vec[:, 8:9]).then_inc(s["wo_ready"], 1)
            per_half(weigh_o)

            def x2_copy(half):
                act.wait_ge(s["x2_t_ps"], half + 1)
                act.activation(x2_t[:, half, :], ps[4 * half + 1][:], ACT.Copy
                               ).then_inc(s["x2_t_ready"], 1)

            def score_tanh(half):
                act.wait_ge(s["w1_ps"], half + 1)
                act.wait_ge(s["in_small"], 64)
                act.activation(tanh_t[:, half, :], ps[4 * half + 2][0:A_DIM, :], ACT.Tanh,
                               bias=b1v[:, 0:1]).then_inc(s["tanh_ready"], 1)

            def softmax(half):
                act.wait_ge(s["soft_arg"], half + 1)
                act.activation(soft[:, half], scores[:, half], ACT.Exp).then_inc(s["exp_s"], 1)

            def y_copy(half):
                act.wait_ge(s["pooled_ps"], half + 1)
                act.activation(y[:, half, :], ps[4 * half + 1][:], ACT.Copy).then_inc(s["y_ready"], 1)

            def y_high(half):
                act.wait_ge(s["pooled_ps"], half + 1)
                act.activation(y_hi[:, half, :], ps[4 * half + 1][:], ACT.Copy
                               ).then_inc(s["y_hi_ready"], 1)

            x2_copy(0)
            score_tanh(0)
            softmax(0)
            x2_copy(1)
            score_tanh(1)
            y_high(0)
            softmax(1)
            act.wait_ge(s["y_split"], 1)
            y_copy(0)

            def gated(step, b):
                act.wait_ge(s["gu_ready"], step + 1)
                act.activation(silu[:, b, :], gate_ps[b][:], ACT.Silu).then_inc(s["silu_ready"], 1)

            def high(half, buf):
                act.activation(hid_hi[buf][:], hid[:, half, :], ACT.Copy).then_inc(s["hid_hi_ready"], 1)

            gated(0, 0)
            act.wait_ge(s["hid_ready"], 1)
            high(0, 0)
            y_copy(1)
            y_high(1)
            gated(1, 1)
            act.wait_ge(s["hid_ready"], 2)
            high(1, 1)
            act.wait_ge(s["logit_in"], 1)
            act.activation(gate_e[:, 1], gate_e[:, 0], ACT.Silu).then_inc(s["silu_l"], 1)
            gated(2, 0)
            gated(3, 1)
            act.wait_ge(s["hid_ready"], 3)
            high(0, 2)

            def route_copy():
                for half in range(HALVES):
                    act.wait_ge(s["route_t_ps"], half + 1)
                    act.activation(route_t[:, half, :], bc_ps[half][0:LO + E_ALL, :], ACT.Copy
                                   ).then_inc(s["route_t_ready"], 1)

            def body(i, first=False):
                for u in range(BODY_STEPS):
                    n = i * BODY_STEPS + (u + HALVES * PLAIN)
                    gated(n, u % 2)
                    if first and u == 1:
                        route_copy()
                    act.wait_ge(s["hid_ready"], n)
                    if not (first and u == 0):
                        act.wait_ge(s["bc_used"], n - 4)
                    high((u + 1) % 2, (u + 3) % HID_BUFS)

            body(0, True)
            with act.Fori(1, TURNS) as i:
                body(i)
            act.wait_ge(s["bc_used"], STEPS - HALVES * PLAIN)
            act.wait_ge(s["weight_used"], CHUNKS - 2)
            buf = (STEPS - 1) % HID_BUFS
            for part in PARTS:
                act.activation(hid_hi[buf][:, part], hid[:, 1, part], ACT.Copy
                               ).then_inc(s["hid_hi_ready"], 1)
            act.wait_ge(s["acc_ready"], 1)
            act.activation(acc_sb[:, 0, :], acc_ps[0][:], ACT.Copy).then_inc(s["acc_out"], 1)
            act.wait_ge(s["last_down"], 2)
            for part in PARTS:
                act.activation(acc_sb[:, 1, part], acc_ps[1][:, part], ACT.Copy).then_inc(s["acc_out"], 1)

        @block.vector
        def _(v):
            step = [0]

            def then(ins):
                step[0] += 1
                ins.then_inc(s["vec_step"], 1)
                v.wait_ge(s["vec_step"], step[0])

            def weight_sums():
                v.wait_ge(s["in_aw"], 16)
                v.tensor_reduce(abs_sum[:], aw[:], AX_X, ALU.add, apply_absolute_value=True
                                ).then_inc(s["abs_ready"], 1)

            def note(ins):
                step[0] += 1
                ins.then_inc(s["vec_step"], 1)
                return step[0]

            gather("vector", mybir.EngineType.DVE, v, v.tensor_copy)
            weight_sums()
            v.wait_ge(s["in_vec"], 16)
            v.tensor_scalar(one_less[:], vec[:, 2:5], -1.0, 1.0, ALU.mult, ALU.add
                            ).then_inc(s["one_less_done"], 1)
            v.wait_ge(s["decay_done"], 1)
            v.tensor_scalar(log_w[:], decay[:], -1.0, None, ALU.mult).then_inc(s["log_w_ready"], 1)
            v.wait_ge(s["log_w_ready"], 1)
            v.wait_ge(s["const_ready"], 10)
            then(v.tensor_scalar(scan_w[:, :, 1:TP], h_pad[:, 0, :, 0:1].broadcast_to([P, HB, T]),
                                 log_w[:, 0:1], None, ALU.add))
            v.memset(scan_w[:, :, 0:1], -BIG).then_inc(s["scan_ready"], 1)
            def per_half(f):
                for half in range(HALVES):
                    f(half)

            def h_out(half):
                v.wait_ge(s["h_ps"], half + 1)
                v.tensor_tensor(h_pad[:, half, :, 1:TP], steps(ps[4 * half][:]),
                                cond_w[:, half * HB:(half + 1) * HB, D:D + 1].broadcast_to([P, HB, T]),
                                ALU.add).then_inc(s["h_ready"], 1)

            def mix(half):
                v.wait_ge(s["h_ready"], half + 1)
                for m in range(3):
                    v.wait_ge(s["shift_ready"], 3 * half + m + 1)
                    v.scalar_tensor_tensor(out=steps(mixed[:, half, m, :]), in0=h_pad[:, half, :, 1:TP],
                                           scalar=vec[:, 2 + m:3 + m], in1=steps(shifted[:, half, m, :]),
                                           op0=ALU.mult, op1=ALU.add).then_inc(s["mix_ready"], 1)

            def weigh(half):
                v.wait_ge(s["mix_ready"], 3 * half + 1)
                v.tensor_scalar(weighted[:, half, 0, :], mixed[:, half, 0, :], vec[:, 5:6],
                                None, ALU.mult).then_inc(s["weighted_ready"], 1)
            v.wait_ge(s["tot_ready"], 1)
            v.tensor_scalar(w_mean[:], ps[7][:, 0:4], 1.0 / (D * D), TINY, ALU.mult, ALU.max
                            ).then_inc(s["w_mean_ready"], 1)
            v.wait_ge(s["w_mean_ready"], 1)
            then(v.reciprocal(w_scale[:], w_mean[:]))
            v.tensor_scalar(w_back[:], w_mean[:], 1.0 / 127.0, None, ALU.mult).then_inc(s["back_ready"], 1)
            for m in range(4):
                last = v.tensor_scalar(w_round[:, m, :], aw[:, m, :], w_scale[:, m:m + 1], ROUND,
                                       ALU.mult, ALU.add)
            rounded = note(last)
            h_out(0)
            mix(0)
            h_out(1)
            weigh(0)
            mix(1)
            weigh(1)

            def mean_squares(half, n, sumsq, meansq_sem):
                v.wait_ge(sumsq[0], half + 1)
                v.tensor_scalar(stat[:, half, 0, 0:n], sumsq[1], 1.0 / D, RMS_EPS, ALU.mult, ALU.add
                                ).then_inc(meansq_sem, 1)

            def peaks(half, n, turned):
                for m in range(n // HT):
                    v.wait_ge(turned, n // HT * half + m + 1)
                    last = v.tensor_reduce(stat[:, half, 2, HT * m:HT * m + HT],
                                           tiles(ps[4 * half + 1 + m][:]), AX_X, ALU.max,
                                           apply_absolute_value=True)
                then(last)

            def scale_rows(half, n, rms_sem, back_w, done):
                st = stat[:, half]
                v.wait_ge(rms_sem, half + 1)
                then(v.tensor_tensor(st[:, 3, 0:n], st[:, 2, 0:n], st[:, 1, 0:n], ALU.mult))
                then(v.tensor_scalar(st[:, 4, 0:n], st[:, 3, 0:n], TINY, None, ALU.max))
                then(v.reciprocal(st[:, 5, 0:n], st[:, 4, 0:n]))
                v.scalar_tensor_tensor(out=st[:, 6, 0:n], in0=st[:, 1, 0:n], scalar=127.0,
                                       in1=st[:, 5, 0:n], op0=ALU.mult, op1=ALU.mult).then_inc(done, 1)
                v.tensor_tensor(st[:, 7, 0:n].rearrange("p (m n) -> p m n", n=HT),
                                st[:, 4, 0:n].rearrange("p (m n) -> p m n", n=HT), back_w,
                                ALU.mult).then_inc(done, 1)

            for half in range(HALVES):
                mean_squares(half, 3 * HT, (s["sumsq_ready"], ps[4 * half][:, 0:3 * HT]),
                             s["meansq_ready"])
                peaks(half, 3 * HT, s["weighted_t"])
                if half == 0:
                    v.wait_ge(s["vec_step"], rounded)
                    then(v.tensor_scalar(w_clip, w_round, -ROUND, 1.0, ALU.add, ALU.min))
                    v.tensor_scalar(w_q[:], w_clip, -1.0, None, ALU.max).then_inc(s["w_q_ready"], 1)
            v.wait_ge(s["back_ready"], 1)
            for half in range(HALVES):
                scale_rows(half, 3 * HT, s["rms_ready"],
                           w_back[:, 0:3].unsqueeze(2).broadcast_to([P, 3, HT]), s["scale_ready"])

            def quantise(half):
                got = [0] * 3
                for m in range(4):
                    if m < 3:
                        v.wait_ge(s["scale_bc"], 3 * half + m + 1)
                        v.wait_ge(*((s["weighted_vr"], 2 * half + m) if m else
                                    (s["weighted_ready"], half + 1)))
                        got[m] = note(v.tensor_tensor(scaled[:, half, m, :], weighted[:, half, m, :],
                                                      ps[4 * half + 1 + m][:], ALU.mult))
                    if m:
                        v.wait_ge(s["vec_step"], got[m - 1])
                        v.tensor_scalar(quant[:, half, m - 1, :], scaled[:, half, m - 1, :], ROUND, -ROUND,
                                        ALU.add, ALU.add).then_inc(s["quant_ready"], 1)
            per_half(quantise)

            def wkv_args(half):
                v.wait_ge(s["proj_ready"], 3 * half + 1)
                v.wait_ge(s["back_sb"], 3 * half + 1)
                v.tensor_tensor(k_pad[:, half, :, 1:TP], steps(ps[4 * half + 1][:]),
                                steps(back[:, half, 0, :]), ALU.mult).then_inc(s["k_ready"], 1)
                v.wait_ge(s["k_ready"], half + 1)
                v.wait_ge(s["scan_ready"], 1)
                flat = "p b t -> p (b t)"
                v.tensor_tensor_scan(eps[:, half].rearrange(flat), scan_w[:].rearrange(flat),
                                     k_pad[:, half].rearrange(flat), 0.0, ALU.add, ALU.max
                                     ).then_inc(s["eps_ready"], 1)
                v.wait_ge(s["eps_ready"], half + 1)
                old, k = eps[:, half, :, 0:T], k_pad[:, half, :, 1:TP]
                v.scalar_tensor_tensor(out=steps(lead[:, half, :]), in0=k, scalar=vec[:, 1:2], in1=old,
                                       op0=ALU.add, op1=ALU.subtract).then_inc(s["lead_ready"], 1)
                v.wait_ge(s["lead_ready"], half + 1)
                v.tensor_scalar(arg[:, half, 1, :], lead[:, half, :], 0.0, None, ALU.min
                                ).then_inc(s["new_u_arg_ready"], 1)
                v.wait_ge(s["proj_ready"], 3 * half + 3)
                v.wait_ge(s["back_sb"], 3 * half + 3)
                v.tensor_tensor(rec[:, half, :], ps[4 * half + 3][:], back[:, half, 2, :], ALU.mult
                                ).then_inc(s["r_ready"], 1)
                v.tensor_tensor(val[:, half, :], ps[4 * half + 2][:], back[:, half, 1, :], ALU.mult
                                ).then_inc(s["val_ready"], 1)
            per_half(wkv_args)

            def wkv_sums(half):
                flat = "p b t -> p (b t)"
                v.wait_ge(s["new_ready"], half + 1)
                v.wait_ge(s["dec_ready"], half + 1)
                got_beta = note(v.tensor_tensor_scan(
                    beta[:, half].rearrange(flat), dec_pad[:, half].rearrange(flat),
                    new_pad[:, half].rearrange(flat), 0.0, ALU.mult, ALU.add))
                v.wait_ge(s["newv_ready"], half + 1)
                v.tensor_tensor_scan(
                    alpha[:, half].rearrange(flat), dec_pad[:, half].rearrange(flat),
                    newv_pad[:, half].rearrange(flat), 0.0, ALU.mult, ALU.add
                    ).then_inc(s["alpha_ready"], 1)
                v.wait_ge(s["e1_ready"], half + 1)
                v.wait_ge(s["e2_ready"], half + 1)
                pr = prod[:, half]
                e1, e2 = e12[:, half, 0, :], e12[:, half, 1, :]
                v.wait_ge(s["vec_step"], got_beta)
                then(v.tensor_tensor(steps(pr[:, 0, :]), steps(e1), beta[:, half, :, 0:T], ALU.mult))
                weight = note(v.tensor_tensor(pr[:, 0, :], pr[:, 0, :], e2, ALU.add))
                v.wait_ge(s["vec_step"], weight)
                v.wait_ge(s["exp_r_ready"], half + 1)
                return note(v.scalar_tensor_tensor(out=pr[:, 3, :], in0=exp_r[:, half, :], scalar=1.0,
                                                   in1=pr[:, 0, :], op0=ALU.add, op1=ALU.mult))

            def wkv_quotient(half, divisor):
                pr = prod[:, half]
                v.wait_ge(s["vec_step"], divisor)
                then(v.reciprocal(pr[:, 0, :], pr[:, 3, :]))
                v.wait_ge(s["numerator_ready"], half + 1)
                v.tensor_tensor(mixed_o[:, half, :], pr[:, 1, :], pr[:, 0, :], ALU.mult
                                ).then_inc(s["o_ready"], 1)

            def mean_squares_o(half):
                mean_squares(half, HT, (s["sumsq_o"], ps[4 * half][:, 0:HT]), s["meansq_o"])

            def scale_rows_o(half):
                scale_rows(half, HT, s["rms_o"], w_back[:, 3:4].unsqueeze(2).broadcast_to([P, 1, HT]),
                           s["scale_o"])

            def quantise_o(half):
                v.wait_ge(s["bc_o"], half + 1)
                then(v.tensor_tensor(scaled[:, half, 0, :], weighted[:, half, 0, :],
                                     ps[4 * half + 2][:], ALU.mult))
                v.tensor_scalar(quant[:, half, 0, :], scaled[:, half, 0, :], ROUND, -ROUND,
                                ALU.add, ALU.add).then_inc(s["quant_o"], 1)

            def residual(half):
                v.wait_ge(s["out_ps"], half + 1)
                v.wait_ge(s["in_x"], 16)
                for n in range(HT):
                    t = half * HT + n
                    last = v.scalar_tensor_tensor(out=x2[:, t, :], in0=ps[4 * half + 3][:, n * D:(n + 1) * D],
                                                  scalar=stat[:, half, 7, n:n + 1], in1=x_tok[:, t, :],
                                                  op0=ALU.mult, op1=ALU.add)
                last.then_inc(s["x2_ready"], 1)

            wkv_quotient(0, wkv_sums(0))
            divisor = wkv_sums(1)
            mean_squares_o(0)
            peaks(0, HT, s["wo_t"])
            scale_rows_o(0)
            wkv_quotient(1, divisor)
            quantise_o(0)
            residual(0)
            mean_squares_o(1)
            peaks(1, HT, s["wo_t"])
            scale_rows_o(1)
            v.wait_ge(s["penalty_ready"], 1)
            v.tensor_reduce(count[:], mask[:], AX_X, ALU.add).then_inc(s["count_ready"], 1)
            quantise_o(1)

            def soft_in(half):
                v.wait_ge(s["score_ps"], half + 1)
                then(v.tensor_tensor(scores[:, half], tiles(ps[4 * half][:, 0:HT * T]),
                                     penalty[:, half * HT:(half + 1) * HT, :], ALU.add))
                return note(v.tensor_reduce(row[:, half, 0, :], scores[:, half], AX_X, ALU.max))

            def soft_shift(half, peak):
                v.wait_ge(s["vec_step"], peak)
                v.tensor_tensor(scores[:, half], scores[:, half],
                                row[:, half, 0, :].unsqueeze(2).broadcast_to([P, HT, T]), ALU.subtract
                                ).then_inc(s["soft_arg"], 1)

            def soft_out(half):
                v.wait_ge(s["exp_s"], half + 1)
                v.wait_ge(s["count_ready"], 1)
                then(v.tensor_reduce(row[:, half, 1, :], soft[:, half], AX_X, ALU.add))
                then(v.tensor_tensor(row[:, half, 2, :], row[:, half, 1, :],
                                     count[:, half * HT:(half + 1) * HT], ALU.mult))
                then(v.reciprocal(row[:, half, 3, :], row[:, half, 2, :]))
                then(v.tensor_tensor(soft_n[:, half], soft[:, half],
                                     row[:, half, 3, :].unsqueeze(2).broadcast_to([P, HT, T]), ALU.mult))
                for g in range(4):
                    r = slice(32 * g, 32 * g + 32)
                    last = v.transpose(blocks[r, half, :, 32 * g:32 * g + 32], soft_n[r, half])
                last.then_inc(s["blocks_ready"], 1)

            peak = soft_in(0)
            residual(1)
            soft_shift(0, peak)

            def y_low(half, of):
                v.wait_ge(s["y_hi_ready"], half + 1)
                v.tensor_tensor(y_lo[:, half, :], of, y_hi[:, half, :].bitcast(F32),
                                ALU.subtract).then_inc(s["y_split"], 1)
            soft_out(0)
            soft_shift(1, soft_in(1))
            y_low(0, ps[1][:])
            soft_out(1)
            wide = [P, TILES, E_ROUTED]
            ge, gt = gate_e, gate_t

            def over(k):
                return gt[:, k, :].unsqueeze(2).broadcast_to(wide)
            rk = rank[:].unsqueeze(1).broadcast_to(wide)
            def product(n, half):
                v.wait_ge(s["silu_ready"], n + 1)
                if not isinstance(n, int) or n > 1:
                    v.wait_ge(s["hid_split"], n - 1)
                v.tensor_tensor(hid[:, half, :], silu[:, half, :], up_ps[half][:], ALU.mult
                                ).then_inc(s["hid_ready"], 1)

            def low(n, half, buf):
                v.wait_ge(s["hid_hi_ready"], n + 1)
                v.tensor_tensor(hid_lo[buf][:], hid[:, half, :], hid_hi[buf][:].bitcast(F32),
                                ALU.subtract).then_inc(s["hid_split"], 1)

            product(0, 0)
            low(0, 0, 0)
            v.wait_ge(s["y_ready"], 2)
            y_low(1, y[:, 1, :])
            product(1, 1)
            v.wait_ge(s["logit_ps"], 2)
            then(v.tensor_tensor(ge[:, 2], ps[4][:, 0:TILES * E_ROUTED].rearrange(
                "p (n e) -> p n e", n=TILES), rbias[:].unsqueeze(1).broadcast_to(wide), ALU.mult))
            then(v.tensor_scalar(ge[:, 3], ge[:, 2], 0.0, 2 * NEAR_ZERO, ALU.is_ge, ALU.mult))
            v.scalar_tensor_tensor(out=ge[:, 0], in0=ge[:, 3], scalar=-NEAR_ZERO, in1=ge[:, 2],
                                   op0=ALU.add, op1=ALU.add).then_inc(s["logit_in"], 1)
            v.wait_ge(s["logit_in"], 1)
            over_x = note(v.reciprocal(ge[:, 2], ge[:, 0]))
            low(1, 1, 1)
            v.wait_ge(s["vec_step"], over_x)
            v.wait_ge(s["silu_l"], 1)
            then(v.tensor_tensor(ge[:, 3], ge[:, 1], ge[:, 2], ALU.mult))

            def largest(k, probs):
                then(v.tensor_reduce(gt[:, k, :], ge[:, probs], AX_X, ALU.max))
                then(v.tensor_tensor(ge[:, 4], ge[:, probs], over(k), ALU.is_equal))
                return note(v.tensor_tensor(ge[:, 4], ge[:, 4], rk, ALU.mult))

            ranked = largest(0, 3)
            product(2, 0)
            v.wait_ge(s["vec_step"], ranked)
            then(v.tensor_reduce(gt[:, 2, :], ge[:, 4], AX_X, ALU.max))
            then(v.tensor_tensor(ge[:, 5], rk, over(2), ALU.is_equal))
            without = note(v.scalar_tensor_tensor(out=ge[:, 6], in0=ge[:, 5], scalar=-2.0, in1=ge[:, 3],
                                                  op0=ALU.mult, op1=ALU.add))
            v.wait_ge(s["vec_step"], without)
            ranked = largest(1, 6)
            product(3, 1)
            total = note(v.tensor_tensor(gt[:, 4, :], gt[:, 0, :], gt[:, 1, :], ALU.add))
            v.wait_ge(s["vec_step"], ranked)
            where = note(v.tensor_reduce(gt[:, 3, :], ge[:, 4], AX_X, ALU.max))
            v.wait_ge(s["vec_step"], total)
            inverse = note(v.reciprocal(gt[:, 5, :], gt[:, 4, :]))
            v.wait_ge(s["vec_step"], where)
            second = note(v.tensor_tensor(ge[:, 7], rk, over(3), ALU.is_equal))
            v.wait_ge(s["vec_step"], inverse)
            shares = note(v.tensor_tensor(ge[:, 0], ge[:, 3], over(5), ALU.mult))
            v.wait_ge(s["vec_step"], second)
            then(v.tensor_tensor(ge[:, 5], ge[:, 5], ge[:, 7], ALU.add))
            v.wait_ge(s["vec_step"], shares)
            v.wait_ge(s["one_ready"], 1)
            note(v.tensor_tensor(route[:, :, 1:E_ALL], ge[:, 5], ge[:, 0], ALU.mult))
            then(v.tensor_tensor(ge[:, 6], ge[:, 5], ge[:, 0], ALU.mult))
            v.tensor_tensor(route[:, :, LO + 1:], ge[:, 6], route[:, :, 1:E_ALL].bitcast(F32), ALU.subtract
                            ).then_inc(s["route_ready"], 1)
            low(2, 0, 2)

            def body(i):
                for u in range(BODY_STEPS):
                    half = u % 2
                    n = i * BODY_STEPS + (u + HALVES * PLAIN)
                    product(n, half)
                    low(n - 1, 1 - half, (u + 3) % HID_BUFS)
                    v.wait_ge(s["bc_ready"], i * SPREADS + (u + 1 if u < 2 else u - 1))
                    v.wait_ge(s["hid_ready"], n + 1)
                    v.tensor_tensor(hid[:, half, :], hid[:, half, :], bc_ps[half][:], ALU.mult
                                    ).then_inc(s["bc_used"], 1)

            with v.Fori(0, TURNS) as i:
                body(i)
            buf = (STEPS - 1) % HID_BUFS
            for k, part in enumerate(PARTS):
                v.wait_ge(s["hid_hi_ready"], STEPS + k)
                v.tensor_tensor(hid_lo[buf][:, part], hid[:, 1, part], hid_hi[buf][:, part].bitcast(F32),
                                ALU.subtract).then_inc(s["hid_split"], 1)

            def add_residual(bank, turned, first, end):
                v.wait_ge(s["out_t"], turned)
                v.tensor_tensor(final[:, first:end, :], tiles(bank[:])[:, first % HT:first % HT + end - first, :],
                                x2[:, first:end, :], ALU.add).then_inc(s["out_ready"], 1)

            add_residual(ps[0], 1, 0, HT)
            add_residual(ps[1], 2, HT, HT + HT // 2)
            add_residual(ps[2], 3, HT + HT // 2, TILES)

        @block.tensor
        def _(pe):
            def per_half(f):
                for half in range(HALVES):
                    f(half)

            def spread(bank, column):
                for n in range(HT):
                    last = pe.transpose(bank[:, n * P:(n + 1) * P], lane(column(n), P), ident[:])
                return last

            def keep_warm(bank, count):
                for _ in range(count):
                    pe.matmul(bank[:], zeros[:, 0:P], zeros[:], start=True, stop=True)

            pe.wait_ge(s["zeros_ready"], 1)
            keep_warm(ps[6], 15)

            def cond_product(half):
                pe.wait_ge(in_xt[half], 16)
                for k, (first, end) in GATHER.items():
                    pe.wait_ge(gathered[k], (half + 1) * (end - first))
                for j in reversed(range(HB)):
                    if half == 0 and j == HB // 2:
                        pe.wait_ge(s["abs_ready"], 1)
                        pe.wait_ge(s["const_ready"], 10)
                        pe.matmul(ps[7][:, 0:4], ones[:], abs_sum[:], start=True, stop=True
                                  ).then_inc(s["tot_ready"], 1)
                    b, j0 = half * HB + j, max(0, j + 1 - WIDE // T)
                    last = pe.matmul(ps[4 * half][:, j0 * T:(j + 1) * T], cond_w[:, b, 0:D],
                                     x_ch[:, half * HB + j0:b + 1, :], start=True, stop=True)
                last.then_inc(s["h_ps"], 1)
            per_half(cond_product)
            pe.wait_ge(s["ident_ready"], 1)

            def sum_squares(bank, column, squares):
                for n in range(HT):
                    at = column + n
                    last = pe.matmul(bank[:, at:at + WIDE], squares[:, n * P:(n + 1) * P],
                                     ones[:, 0:WIDE], start=True, stop=True)
                return last

            def turn(half):
                for m in range(3):
                    pe.wait_ge(s["square_ready"], 3 * half + m + 1)
                    last = sum_squares(ps[4 * half], m * HT, square[:, half, m, :])
                    if m == 2:
                        last.then_inc(s["sumsq_ready"], 1)
                    pe.wait_ge(*((s["weighted_vr"], 2 * half + m) if m else
                                 (s["weighted_ready"], half + 1)))
                    for n in range(HT):
                        last = pe.transpose(ps[4 * half + 1 + m][:, n * P:(n + 1) * P],
                                            weighted[:, half, m, n * P:(n + 1) * P], ident[:])
                    last.then_inc(s["weighted_t"], 1)
            turn(0)
            pe.wait_ge(s["w_mean_ready"], 1)
            turn(1)
            pe.wait_ge(s["meansq_ready"], 1)
            keep_warm(ps[0], 8)

            def scale_out(half):
                pe.wait_ge(s["scale_ready"], 2 * half + 2)
                for m in range(3):
                    spread(ps[4 * half + 1 + m],
                           lambda n: stat[:, half, 6, m * HT + n:m * HT + n + 1]
                           ).then_inc(s["scale_bc"], 1)
            per_half(scale_out)

            def project(half):
                pe.wait_ge(s["w_q_ready"], 1)
                for m in range(3):
                    if m:
                        pe.wait_ge(s["back_sb"], 3 * half + m)
                    spread(ps[4 * half], lambda n: stat[:, half, 7, m * HT + n:m * HT + n + 1]
                           ).then_inc(s["back_bc"], 1)
                    pe.wait_ge(s["quant_ready"], 3 * half + m + 1)
                    pe.matmul(ps[4 * half + 1 + m][:], w_q[:, m, :], quant[:, half, m, :],
                              start=True, stop=True).then_inc(s["proj_ready"], 1)
            per_half(project)

            def turn_o(half):
                pe.wait_ge(s["sq_o"], half + 1)
                sum_squares(ps[4 * half], 0, square[:, half, 0, :]).then_inc(s["sumsq_o"], 1)
                pe.wait_ge(s["wo_ready"], half + 1)
                for n in range(HT):
                    last = pe.transpose(ps[4 * half + 1][:, n * P:(n + 1) * P],
                                        weighted[:, half, 0, n * P:(n + 1) * P], ident[:])
                last.then_inc(s["wo_t"], 1)

            def scale_out_o(half):
                pe.wait_ge(s["scale_o"], 2 * half + 2)
                spread(ps[4 * half + 2], lambda n: stat[:, half, 6, n:n + 1]).then_inc(s["bc_o"], 1)

            def project_o(half):
                pe.wait_ge(s["quant_o"], half + 1)
                for n in range(HT):
                    last = pe.matmul(ps[4 * half + 3][:, n * D:(n + 1) * D],
                                     quant[:, half, 0, n * P:(n + 1) * P], w_q[:, 3, :],
                                     start=True, stop=True)
                last.then_inc(s["out_ps"], 1)

            def x2_turn(half):
                pe.wait_ge(s["x2_ready"], half + 1)
                for n in range(HT):
                    last = pe.transpose(ps[4 * half + 1][:, n * P:(n + 1) * P], x2[:, half * HT + n, :],
                                        ident[:])
                last.then_inc(s["x2_t_ps"], 1)
            def score(half):
                pe.wait_ge(s["in_small"], 64)
                pe.wait_ge(s["x2_t_ready"], half + 1)
                pe.matmul(ps[4 * half + 2][0:A_DIM, :], w1_sb[:], x2_t[:, half, :], start=True, stop=True
                          ).then_inc(s["w1_ps"], 1)

            def score_rows(half):
                pe.wait_ge(s["tanh_ready"], half + 1)
                for g in range(4):
                    last = pe.matmul(tiles(ps[4 * half][32 * g:32 * g + 32, 0:HT * T]),
                                     b1v[:, 1:2].broadcast_to([A_DIM, T]),
                                     tiles(tanh_t[:, half, :])[:, :, 32 * g:32 * g + 32],
                                     start=True, stop=True)
                last.then_inc(s["score_ps"], 1)

            def pooled(half):
                pe.wait_ge(s["blocks_ready"], half + 1)
                for n in range(HT):
                    last = pe.matmul(ps[4 * half + 1][:, n * P:(n + 1) * P], x2[:, half * HT + n, :],
                                     blocks[:, half, n, :], start=True, stop=True)
                last.then_inc(s["pooled_ps"], 1)

            turn_o(0)
            scale_out_o(0)
            keep_warm(ps[7], 8)
            project_o(0)
            turn_o(1)
            x2_turn(0)
            score(0)
            scale_out_o(1)
            keep_warm(ps[7], 5)
            score_rows(0)
            project_o(1)
            keep_warm(ps[6], 2)
            x2_turn(1)
            keep_warm(ps[6], 3)
            score(1)
            keep_warm(ps[4], 1)
            pooled(0)
            score_rows(1)
            def three(bank, lhs, rhs, start, stop):
                for k, (a, b) in enumerate(((0, 0), (0, 1), (1, 0))):
                    last = pe.matmul(bank, lhs[a], rhs[b], start=start and k == 0, stop=stop and k == 2,
                                     skip_group_check=not start)
                return last

            def part(buf, which):
                at = slice(which * P, (which + 1) * P)
                return w_hi[buf][:, at], w_lo[buf][:, at]

            def gate_up(n, buf, half):
                b = buf % 2 if isinstance(n, int) and n < HALVES * PLAIN else half
                y_parts = (y_hi[:, half, :], y_lo[:, half, :])
                if not isinstance(n, int) or n > 1:
                    pe.wait_ge(s["hid_ready"], n - 1)
                three(gate_ps[b][:], part(buf, 0), y_parts, True, True)
                three(up_ps[b][:], part(buf, 1), y_parts, True, True).then_inc(s["gu_ready"], 1)

            def down(n, buf, half, hid_buf, stop=False):
                pe.wait_ge(s["hid_split"], n + 1)
                return three(acc_ps[half][:], part(buf, 2), (hid_hi[hid_buf][:], hid_lo[hid_buf][:]),
                             False, stop)

            def logits(half):
                pe.wait_ge(s["y_ready"], half + 1)
                if half == 0:
                    pe.wait_ge(s["soft_arg"], 2)
                for n in range(HT):
                    at = (half * HT + n) * E_ROUTED
                    last = pe.matmul(ps[4][:, at:at + WIDE], y[:, half, n * P:(n + 1) * P], wr[:],
                                     start=True, stop=True)
                last.then_inc(s["logit_ps"], 1)
            keep_warm(ps[6], 4)
            for half in range(HALVES):
                pe.matmul(acc_ps[half][:], zeros[:, 0:P], zeros[:], start=True, stop=False,
                          skip_group_check=True)
            pe.wait_ge(s["y_split"], 1)
            pe.wait_ge(s["weight_split"], 1)
            gate_up(0, 0, 0)
            logits(0)
            pooled(1)
            pe.wait_ge(s["weight_split"], 2)
            gate_up(1, 1, 0)
            logits(1)
            pe.wait_ge(s["y_split"], 2)
            gate_up(2, 0, 1)
            gate_up(3, 1, 1)
            down(0, 0, 0, 0)
            def out_turn(bank, half, first, end):
                for n in range(first, end):
                    last = pe.transpose(bank[:, n * P:(n + 1) * P], acc_sb[:, half, n * P:(n + 1) * P],
                                        ident[:])
                last.then_inc(s["out_t"], 1)

            def turn_route():
                pe.wait_ge(s["y_hi_ready"], 2)
                pe.wait_ge(s["route_ready"], 1)
                for half in range(HALVES):
                    for t in range(HT):
                        last = pe.transpose(bc_ps[half][0:LO + E_ALL, t * P:(t + 1) * P],
                                            route[:, half * HT + t, :].bitcast(F32), ident[:])
                    last.then_inc(s["route_t_ps"], 1)

            def weight_rows(i, u):
                half, c, n = u % 2, u // 2, i * BODY_STEPS + (u + HALVES * PLAIN)
                if isinstance(n, int) and u < 2:
                    pe.wait_ge(s["route_t_ready"], half + 1)
                else:
                    pe.wait_ge(s["bc_used"], n - 5)
                pe.wait_ge(s["owner_ready"], i * BODY + (c + 1))
                pe.matmul(bc_ps[half][:], owner[:, (c + PLAIN) % BODY, :], route_t[:, half, :],
                          start=True, stop=True).then_inc(s["bc_ready"], 1)

            def body(i, first=False):
                for u in range(BODY_STEPS):
                    half, c, n = u % 2, u // 2, i * BODY_STEPS + (u + HALVES * PLAIN)
                    before = u + HALVES * PLAIN - LAG
                    if half == 0:
                        pe.wait_ge(s["weight_split"], i * BODY + (c + PLAIN + 1))
                    gate_up(n, (c + PLAIN) % BODY, half)
                    chunk_d, half_d = before // 2, before % 2
                    if first and before < HALVES * PLAIN:
                        chunk_d, half_d = before % 2, before // 2
                    if first and u == 1:
                        turn_route()
                    last = down(n - LAG, chunk_d % BODY, half_d, before % HID_BUFS)
                    if half_d:
                        last.then_inc(s["weight_used"], 1)
                    if first and u == 1:
                        weight_rows(i, 0)
                        weight_rows(i, 1)
                    elif c != 1 and not (first and u == 0):
                        weight_rows(i, u)

            body(0, True)
            with pe.Fori(1, TURNS) as i:
                body(i)
            for n in range(STEPS - LAG, STEPS - 1):
                last = down(n, (n // 2) % BODY, n % 2, n % HID_BUFS, n == STEPS - 2)
            last.then_inc(s["acc_ready"], 1)
            hid_buf = (STEPS - 1) % HID_BUFS
            for k, cols in enumerate(PARTS):
                pe.wait_ge(s["hid_split"], STEPS + k)
                three(acc_ps[1][:, cols], part((CHUNKS - 1) % BODY, 2),
                      (hid_hi[hid_buf][:, cols], hid_lo[hid_buf][:, cols]), False, True
                      ).then_inc(s["last_down"], 1)
            pe.wait_ge(s["acc_out"], 1)
            out_turn(ps[0], 0, 0, HT)
            pe.wait_ge(s["acc_out"], 2)
            out_turn(ps[1], 1, 0, HT // 2)
            pe.wait_ge(s["acc_out"], 3)
            out_turn(ps[2], 1, HT // 2, HT)


def kernel(**inputs):
    import numpy as np
    import concourse.bacc as bacc
    from concourse.bass_utils import run_bass_kernel_spmd as run

    a = {k: np.asarray(v) for k, v in inputs.items()}
    attn = [a["L0_attn_" + n] for n in ("w_key", "w_value", "w_receptance", "w_output")]

    def experts_of(kind):
        return np.concatenate([a["L0_ffn_shared_" + kind][None], a["L0_ffn_routed_" + kind]])

    quarters = [(e, q) for e in range(E_ALL) for q in range(PER_EXPERT)]
    full = [(e, q) for e in range(TURNS + 1) for q in range(PLAIN * QUARTERS)]
    others = [eq for eq in quarters if eq not in full]
    order = full[:PLAIN * QUARTERS]
    for i in range(TURNS):
        for some, count in ((full[PLAIN * QUARTERS:], PLAIN), (others, BODY - PLAIN)):
            order += some[i * count * QUARTERS:(i + 1) * count * QUARTERS]
    index = [e * PER_EXPERT + q for e, q in order]
    owner = np.zeros((LO + E_ALL, len(order) - PLAIN * QUARTERS), np.float32)
    for at, (e, _) in enumerate(order[PLAIN * QUARTERS:]):
        owner[[e, LO + e], at] = 1.0

    def by_chunk(kind):
        w = experts_of(kind).transpose(1, 0, 2).reshape(D, len(quarters), QROWS)[:, index]
        return w.reshape(D, CHUNKS, P).transpose(1, 0, 2)
    down = experts_of("down").reshape(len(quarters), QROWS, D)[index].reshape(CHUNKS, P, D)
    chunks = np.stack([by_chunk("gate"), by_chunk("up"), down], axis=2)
    arrays = {
        "x": a["x"],
        "x_t": a["x"].reshape(B * T, D).T,
        "subject": a["itok_B_0_15"].reshape(1, B),
        "prompt_type": a["itok_B_0_2"].reshape(TILES, 4).T,
        "cond": np.concatenate([a["L0_cond_weights"], a["L0_cond_b"][:, :, None]], axis=2
                               ).transpose(1, 0, 2).reshape(D, SUBJECTS * (D + 1)),
        "cols": np.stack([a["L0_attn_" + n].reshape(D) for n in (
            "time_decay", "time_first", "time_mix_key", "time_mix_value", "time_mix_receptance",
            "rms_key", "rms_value", "rms_receptance", "rms_output")], axis=1),
        "attn_w": np.concatenate([w.T for w in attn], axis=1),
        "w1": a["L0_cond2_W1"],
        "b1_v": np.stack([a["L0_cond2_b1"], a["L0_cond2_v"]], axis=1),
        "router_w": a["L0_ffn_Wr"],
        "router_b": a["L0_ffn_routing_bias"].reshape(1, E_ROUTED),
        "quarter_owner": owner,
        "experts": chunks.reshape(CHUNKS // 2, 2, P, CHUNK_W).transpose(0, 2, 1, 3
                                                                        ).reshape(CHUNKS // 2, P, PACK),
    }
    nc = bacc.Bacc("TRN2", target_bir_lowering=False, num_devices=1)
    feed, args = {}, []
    for name, value in arrays.items():
        value = np.ascontiguousarray(value)
        feed["in_" + name] = value
        args.append(nc.dram_tensor("in_" + name, value.shape, mybir.dt.from_np(value.dtype),
                                   kind="ExternalInput").ap())
    out = nc.dram_tensor("out_0", (B, T, D), F32, kind="ExternalOutput").ap()
    adaln_attention_ffn(nc, *args, out)
    return run(nc, [feed], core_ids=[0]).results[0]["out_0"]
```
